# Optimizing a Trainium2 kernel written in Bass

```python
import numpy as np
import jax
import jax.numpy as jnp

def _softmax(x, axis=-1):
    return jax.nn.softmax(x, axis=axis)

def _gelu(x):
    return jax.nn.gelu(x, approximate=True)

def _silu(x):
    return jax.nn.silu(x)

def _sigmoid(x):
    return jax.nn.sigmoid(x)

def _layernorm(x, axis=-1, eps=1e-05):
    m = jnp.mean(x, axis=axis, keepdims=True)
    v = jnp.var(x, axis=axis, keepdims=True)
    return (x - m) / jnp.sqrt(v + eps)

def _scatter_add(tgt, idx, src, axis=0):
    return tgt.at[idx].add(src)

def _segment_sum(src, seg, n):
    return jax.ops.segment_sum(src, seg, n)
kernel_name = 'mk_macaron_d1_jaxref_r8_b4f904'

def setup_inputs(seed: int=0):
    np.random.seed(seed)
    _w = jnp.asarray

    def _L0_attn_setup():
        import jax, jax.numpy as jnp
        import numpy as np
        B_, T_, D_ = (8, 512, 128)

        def _reference_tuple_inner(u, WA, WB, WAf, WBf, w1, w2, b, Wc):
            bsz, seq_len, _ = u.shape
            xf = jnp.concatenate([u[:, :1], jnp.einsum('btd,ed->bte', u[:, 1:], WB)], axis=1)
            xb = jnp.concatenate([jnp.einsum('btd,ed->bte', u[:, 1:], WBf), u[:, -1:]], axis=1)
            gamma = jax.nn.sigmoid(xf @ w1.T + xb @ w2.T + b)
            y = gamma * (xf + xb) + (1.0 - gamma) * u
            final_output = jax.nn.sigmoid(y @ Wc.T).reshape(bsz, seq_len)
            return (y, gamma, final_output)
        key = jax.random.key(seed)
        ks = jax.random.split(key, 9)
        s = 1.0 / np.sqrt(D_)
        return {'u': jax.random.normal(ks[0], (B_, T_, D_), dtype=jnp.float32), 'WA': jax.random.uniform(ks[1], (D_, D_), jnp.float32, -s, s), 'WB': jax.random.uniform(ks[2], (D_, D_), jnp.float32, -s, s), 'WAf': jax.random.uniform(ks[3], (D_, D_), jnp.float32, -s, s), 'WBf': jax.random.uniform(ks[4], (D_, D_), jnp.float32, -s, s), 'w1': jax.random.uniform(ks[5], (1, D_), jnp.float32, -s, s), 'w2': jax.random.uniform(ks[6], (1, D_), jnp.float32, -s, s), 'b': jnp.zeros((1,), dtype=jnp.float32), 'Wc': jax.random.uniform(ks[7], (1, D_), jnp.float32, -s, s)}
    _L0_attn_in = _L0_attn_setup()

    def _L0_ffn_setup():
        import jax, jax.numpy as jnp
        import numpy as np
        TOP_K = 8
        key = jax.random.key(seed)
        ks = jax.random.split(key, 6)
        B, S, D, F, E = (2, 128, 128, 64, 64)
        x = jax.random.normal(ks[0], (B, S, D), dtype=jnp.float32)
        centroids = jax.random.normal(ks[1], (E, D), dtype=jnp.float32) * 0.05
        expert_biases = jnp.zeros((E,), dtype=jnp.float32)
        Ws_up = jax.random.normal(ks[2], (D, F), dtype=jnp.float32) / np.sqrt(D)
        Ws_down = jax.random.normal(ks[3], (F, D), dtype=jnp.float32) / np.sqrt(F)
        W_up = jax.random.normal(ks[4], (E, D, F), dtype=jnp.float32) / np.sqrt(D)
        W_down = jax.random.normal(ks[5], (E, F, D), dtype=jnp.float32) / np.sqrt(F)
        return {'x': x, 'centroids': centroids, 'expert_biases': expert_biases, 'Ws_up': Ws_up, 'Ws_down': Ws_down, 'W_up': W_up, 'W_down': W_down}
    _L0_ffn_in = _L0_ffn_setup()
    _d = {'L0_attn_u': _L0_attn_in['u'], 'L0_attn_WA': _L0_attn_in['WA'], 'L0_attn_WB': _L0_attn_in['WB'], 'L0_attn_WAf': _L0_attn_in['WAf'], 'L0_attn_WBf': _L0_attn_in['WBf'], 'L0_attn_w1': _L0_attn_in['w1'], 'L0_attn_w2': _L0_attn_in['w2'], 'L0_attn_b': _L0_attn_in['b'], 'L0_attn_Wc': _L0_attn_in['Wc'], 'L0_ffn_centroids': _L0_ffn_in['centroids'], 'L0_ffn_expert_biases': _L0_ffn_in['expert_biases'], 'L0_ffn_Ws_up': _L0_ffn_in['Ws_up'], 'L0_ffn_Ws_down': _L0_ffn_in['Ws_down'], 'L0_ffn_W_up': _L0_ffn_in['W_up'], 'L0_ffn_W_down': _L0_ffn_in['W_down']}
    _x0 = _d['L0_attn_u']
    _d['L0_attn_u'] = jax.random.normal(jax.random.fold_in(jax.random.key(seed), 1), (8, 512, 128), dtype=_x0.dtype)
    del _x0
    return _d

def reference(L0_attn_u, L0_attn_WA, L0_attn_WB, L0_attn_WAf, L0_attn_WBf, L0_attn_w1, L0_attn_w2, L0_attn_b, L0_attn_Wc, L0_ffn_centroids, L0_ffn_expert_biases, L0_ffn_Ws_up, L0_ffn_Ws_down, L0_ffn_W_up, L0_ffn_W_down):

    def _L0_attn_ref(u, WA, WB, WAf, WBf, w1, w2, b, Wc):
        import jax, jax.numpy as jnp
        import numpy as np
        B_, T_, D_ = (8, 512, 128)

        def _reference_tuple_inner(u, WA, WB, WAf, WBf, w1, w2, b, Wc):
            bsz, seq_len, _ = u.shape
            xf = jnp.concatenate([u[:, :1], jnp.einsum('btd,ed->bte', u[:, 1:], WB)], axis=1)
            xb = jnp.concatenate([jnp.einsum('btd,ed->bte', u[:, 1:], WBf), u[:, -1:]], axis=1)
            gamma = jax.nn.sigmoid(xf @ w1.T + xb @ w2.T + b)
            y = gamma * (xf + xb) + (1.0 - gamma) * u
            final_output = jax.nn.sigmoid(y @ Wc.T).reshape(bsz, seq_len)
            return (y, gamma, final_output)
        return _reference_tuple_inner(u, WA, WB, WAf, WBf, w1, w2, b, Wc)[0]

    def _L0_ffn_ref(x, centroids, expert_biases, Ws_up, Ws_down, W_up, W_down):
        import jax, jax.numpy as jnp
        import numpy as np
        TOP_K = 8
        B, S, D = x.shape
        E = centroids.shape[0]
        T = B * S
        xf = x.reshape(T, D)
        shared = jax.nn.silu(xf @ Ws_up) @ Ws_down
        aff = xf @ centroids.T
        biased = aff + expert_biases
        _, idx = jax.lax.top_k(biased, TOP_K)
        sel = jnp.take_along_axis(aff, idx, axis=1)
        w = jax.nn.sigmoid(sel)
        w = w / (jnp.sum(w, axis=-1, keepdims=True) + 1e-08)
        cw = jnp.zeros((T, E), dtype=x.dtype).at[jnp.arange(T)[:, None], idx].add(w)
        h = jax.nn.silu(jnp.einsum('td,edf->etf', xf, W_up))
        y = jnp.einsum('etf,efd->etd', h, W_down)
        routed = jnp.einsum('etd,te->td', y, cw)
        return (shared + routed).reshape(B, S, D)
    x = L0_attn_u
    x = x + 0.5 * _L0_ffn_ref(_layernorm(x, axis=-1), L0_ffn_centroids, L0_ffn_expert_biases, L0_ffn_Ws_up, L0_ffn_Ws_down, L0_ffn_W_up, L0_ffn_W_down)
    x = x + _L0_attn_ref(_layernorm(x, axis=-1), L0_attn_WA, L0_attn_WB, L0_attn_WAf, L0_attn_WBf, L0_attn_w1, L0_attn_w2, L0_attn_b, L0_attn_Wc)
    x = x + 0.5 * _L0_ffn_ref(_layernorm(x, axis=-1), L0_ffn_centroids, L0_ffn_expert_biases, L0_ffn_Ws_up, L0_ffn_Ws_down, L0_ffn_W_up, L0_ffn_W_down)
    return x

_drawn_inputs = setup_inputs


def setup_inputs(seed=0):
    import zlib

    import numpy as np

    out = dict(_drawn_inputs(seed))
    spreads = {'L0_ffn_expert_biases': (0.0, 0.1)}
    factors = {}
    for name, (base, spread) in spreads.items():
        noise = np.random.default_rng([zlib.crc32(name.encode()), seed]).standard_normal(out[name].shape)
        drawn = base * np.exp(spread * noise) if base else spread * noise
        out[name] = jnp.asarray(drawn.astype(out[name].dtype))
    for name, factor in factors.items():
        out[name] = (out[name] * factor).astype(out[name].dtype)
    return out
```

```python
from contextlib import ExitStack

import concourse.bass as bass
from concourse import mybir

B, T, D = 8, 512, 128
E, F, TOPK = 64, 64, 8
P = 128
NB = T // P
R = P // E
NJ = F // R
NT = NJ + 1
HT = T // 2
RING = 5
SLOTS = -(-NT // RING) * RING
LAG = RING + 1
GRING = LAG + 1
ORING = 4
NLOW = (NT // 2 + 1, NT // 2)
AW = D + 2
AS = 256
NPIECE = 4
JP = NJ // NPIECE
LN_EPS = 1e-5
SUM_EPS = 1e-8
TAKEN = -3.0e38


class Phase:

    def __init__(self, p, q, at, prep=None, norm0=None, mid=None, norm2=None, keep=None, post=None, first=False, use=None):
        self.p, self.q, self.at, self.first = p, q, at, first
        self.use = p // 2 if isinstance(p, int) else use
        self.steady_a, self.steady_b = prep is not None and post is not None, prep is not None and mid is not None and norm2 is None
        self.prep, self.norm0, self.mid, self.norm2, self.keep, self.post = prep, norm0, mid, norm2, keep, post


PREP = ("x_t", "x_hi", "x_lo", "aff", "sig", "bias", "max", "take", "gate", "sum", "eps", "inv", "cw", "cw_t", "cw_copy")
MID = ("y_t", "x1", "stat1", "aggr1", "rstd1", "norm1", "xu", "u_t", "u_hi", "u_lo",
       "attn", "tanh", "gamma", "t1", "x2")
NORM0, NORM2 = ("stat0", "aggr0", "rstd0", "norm0"), ("stat2", "aggr2", "rstd2", "norm2")


def places(names, at):
    return dict(zip(names, at))


AT_FIRST = places(PREP, (2, 3, 4, 8, 9, 10, 12, 14, 16, 18, 20, 21, 22, 25, 26))
AT_MID_PREP = {
    "y": 3,
    **places(MID, (5, 6, (7, 8), 9, 9, (10, 11), 12, 13, 14, 14, 16, 17, 17, 17, (18, 19))),
    **places(NORM2, ((20, 20), 21, 21, (22, 22))),
    **places(PREP, (24, 24, 25, 27, 28, 28, 29, 29, 30, 30, 31, 31, 31, 33, 34)),
}
AT_SECOND = {**AT_MID_PREP, "keep": 24, **places(NORM0, ((0, 2), 3, 3, (4, 5)))}
AT_STEADY_A = {
    "y": 3, "y_t": 6, "out": 8, **places(NORM2[1:], (0, 1, (2, 4))),
    **places(PREP, (7, 8, 10, 13, 14, 16, 18, 20, 22, 24, 26, 27, 28, 31, 32)),
    "keep": 11, **places(NORM0, ((12, 14), 16, 17, (28, 30))),
}
AT_STEADY_B = {
    "y": 3,
    **places(PREP, (1, 2, 4, 8, 9, 10, 14, 15, 17, 19, 20, 21, 22, 25, 26)),
    **places(MID, (6, 8, (10, 12), 13, 14, (16, 18), 19, 21, 22, 24, 28, 29, 30, 30, (32, 33))),
    "stat2": (34, 34),
}
AT_LAST = {"y": 3, "y_t": 6, "out": 8, "keep": 9}


def over_phases(eng, phase):
    phase(Phase(0, 0, AT_FIRST, prep=(0, 0, 1), first=True))
    phase(Phase(1, 1, AT_SECOND, mid=0, norm2=0, prep=(1, 2, 0), keep=0, norm0=2))
    phase(Phase(2, 0, AT_STEADY_B, prep=(1, 0, 2), mid=1))
    with eng.Fori(2, B - 1) as c:
        phase(Phase(2 * c - 1, 1, AT_STEADY_A, norm2=c - 1, post=c - 2, prep=(c, 2, c - 1), keep=c - 1, norm0=c + 1, use=c - 1))
        phase(Phase(2 * c, 0, AT_STEADY_B, prep=(c, 0, c + 1), mid=c, use=c))
    c = B - 1
    at = {k: v for k, v in AT_STEADY_A.items() if k not in NORM0}
    phase(Phase(2 * c - 1, 1, at, norm2=c - 1, post=c - 2, prep=(c, 2, c - 1), keep=c - 1))
    phase(Phase(2 * c, 0, AT_MID_PREP, mid=c, norm2=c, prep=(c, 2, c)))
    phase(Phase(2 * c + 1, 1, AT_LAST, post=c - 1, keep=c))


def build(nc, x, ident_in, cent_t, ebias, ws_up, ws_down, w_up, w_down, wb, wb_t, wbf, wbf_t, w1, w2, b_in, out):
    fp32, fp32r = mybir.dt.float32, mybir.dt.float32r
    ALU, ACT, AX = mybir.AluOpType, mybir.ActivationFunctionType, mybir.AxisListType
    ctx = ExitStack()
    with ctx:
        def sb(name, shape, dt=fp32):
            return ctx.enter_context(nc.sbuf_tensor(name, shape, dt))

        def sem(name):
            return ctx.enter_context(nc.semaphore(name))

        wu_raw, wd_raw = sb("wu_raw", [P, NJ, P]), sb("wd_raw", [P, NJ, P])
        wu_hi, wu_lo = sb("wu_hi", [P, NJ, P], fp32r), sb("wu_lo", [P, NJ, P], fp32r)
        wd_hi, wd_lo = sb("wd_hi", [P, NJ, P], fp32r), sb("wd_lo", [P, NJ, P], fp32r)
        SU, SDL, SDH = 0, 3 * F, 3 * F + D
        CE = SDH + D
        A1, A2 = CE + E, CE + E + AW
        I1, I2 = A2 + AW, A2 + 2 * AW
        SW = I2 + AW
        sm_raw = sb("sm_raw", [P, SW])
        sm_hi, sm_lo = sb("sm_hi", [P, SW], fp32r), sb("sm_lo", [P, SW], fp32r)
        wb_sb, wbf_sb = sb("wb_sb", [P, P]), sb("wbf_sb", [P, P])
        ident = sb("ident", [P, P])
        bias_b = sb("bias_b", [P, E])
        b_col, b_half = sb("b_col", [P, 1]), sb("b_half", [P, 1])
        neg_half = sb("neg_half", [P, NB])

        x_hi = [sb(f"x_hi{q}", [P, T], fp32r) for q in range(2)]
        x_lo = [sb(f"x_lo{q}", [P, T], fp32r) for q in range(2)]
        cw = [sb(f"cw{q}", [P, T]) for q in range(2)]
        gated = sb("gated", [P, ORING, T])
        g_hi, g_lo = sb("g_hi", [P, GRING, T], fp32r), sb("g_lo", [P, GRING, T], fp32r)

        x_in, x_res = sb("x_in", [P, NB, D]), sb("x_res", [P, NB, D])
        x1, x2, x2_kept = sb("x1", [P, NB, D]), sb("x2", [P, NB, D]), sb("x2_kept", [P, NB, D])
        out_sb = sb("out_sb", [P, NB, D])
        normed = [sb(f"normed{k}", [P, NB, D]) for k in range(3)]
        xu, t1 = sb("xu", [P, NB, D]), sb("t1", [P, NB, D])
        y_sb = sb("y_sb", [P, T])
        stats = [sb(f"stats{k}", [P, NB, 6]) for k in range(3)]
        mv = [sb(f"mv{k}", [P, NB, 2]) for k in range(3)]
        var_eps = [sb(f"var_eps{k}", [P, NB]) for k in range(3)]
        rstd = [sb(f"rstd{k}", [P, NB]) for k in range(3)]
        th, gamma = sb("th", [P, NB]), sb("gamma", [P, NB])
        u_hi, u_lo = sb("u_hi", [P, T + 2], fp32r), sb("u_lo", [P, T + 2], fp32r)
        e0_hi, e0_lo = sb("e0_hi", [P, P], fp32r), sb("e0_lo", [P, P], fp32r)
        e1_hi, e1_lo = sb("e1_hi", [P, P], fp32r), sb("e1_lo", [P, P], fp32r)
        sig, biased, taken = sb("sig", [P, NB, E]), sb("biased", [P, NB, E]), sb("taken", [P, NB, E])
        top = sb("top", [P, NB, TOPK])
        w_sel, w_dup = sb("w_sel", [P, NB, E]), sb("w_dup", [P, NB, E, R])
        w_sum, w_eps, w_inv = sb("w_sum", [P, NB]), sb("w_eps", [P, NB]), sb("w_inv", [P, NB])

        up = [ctx.enter_context(nc.psum_tensor(f"up{i}", [P, T], fp32)) for i in range(RING)]
        y_ps = ctx.enter_context(nc.psum_tensor("y_ps", [P, T], fp32))
        side = ctx.enter_context(nc.psum_tensor("side", [P, 2 * T], fp32))
        side0, side1 = side[:, 0:T], side[:, T:2 * T]
        att = side[:, :].rearrange("p (n c) -> p n c", c=AS)
        side0_rows = side0.rearrange("p (n d) -> p n d", n=NB)

        small_in = [sem(f"small_in{i}") for i in range(3)]
        wu_in, wd_in = [sem(f"wu_in{i}") for i in range(NPIECE)], [sem(f"wd_in{i}") for i in range(NPIECE)]
        consts_set, v_done, sm_hi_done, sm_lo_done = (sem(s) for s in ("consts_set", "v_done", "sm_hi_done", "sm_lo_done"))
        v_copied, half_b_done = sem("v_copied"), sem("half_b_done")
        w_hi_done, w_lo_done = sem("w_hi_done"), sem("w_lo_done")
        up_done, silu_done, gate_done, hi_done = (sem(s) for s in ("up_done", "silu_done", "gate_done", "hi_done"))
        lo_done = [sem("lo_done_vector"), sem("lo_done_pool")]
        down_done, y_copied, y_turned = sem("down_done"), sem("y_copied"), sem("y_turned")
        x_in_done, x_res_done, out_stored = sem("x_in_done"), sem("x_res_done"), sem("out_stored")
        stat_done, mv_done = [sem(f"stat_done{k}") for k in range(3)], [sem(f"mv_done{k}") for k in range(3)]
        eps_done, rstd_done = [sem(f"eps_done{k}") for k in range(3)], [sem(f"rstd_done{k}") for k in range(3)]
        norm_done = [sem(f"norm_done{k}") for k in range(3)]

        def pair(name):
            return [sem(f"{name}{q}") for q in range(2)]

        x_turned, x_hi_done, x_lo_done, aff_done = pair("x_turned"), pair("x_hi_done"), pair("x_lo_done"), pair("aff_done")
        sig_done, bias_done, top_done, taken_done = pair("sig_done"), pair("bias_done"), pair("top_done"), pair("taken_done")
        sel_done, sum_done, sum_eps_done, inv_done = pair("sel_done"), pair("sum_done"), pair("sum_eps_done"), pair("inv_done")
        dup_done, cw_turned, cw_done = pair("dup_done"), pair("cw_turned"), pair("cw_done")
        x1_done, xu_done, u_turned, u_hi_done, u_lo_done = (sem(s) for s in ("x1_done", "xu_done", "u_turned", "u_hi_done", "u_lo_done"))
        att_done, tanh_done, gamma_done, t1_done = (sem(s) for s in ("att_done", "tanh_done", "gamma_done", "t1_done"))
        x2_done, kept_done, out_done = sem("x2_done"), sem("kept_done"), sem("out_done")

        held, power_set = sem("held"), sem("power_set")

        norm_from = [x_in, x1, x2]
        norm_from_done = [None, x1_done, x2_done]

        def before(t):
            return (0, t) if t >= 0 else (1, t + SLOTS)

        def low_count(ph, t):
            back, t = before(t)
            return NLOW[t % 2] * (ph.p - back) + t // 2 + 1

        def halves(ph, name, t):
            at = ph.at.get(name, ())
            blocks = [n for h, a in enumerate(at) if a == t for n in range(h * NB // 2, (h + 1) * NB // 2)]
            return blocks, bool(blocks) and blocks[-1] == NB - 1

        def width(t):
            return T if t < NJ else HT

        def hold(eng, s, value):
            eng.wait_ge(s, value)
            eng.sem_inc(held, 1)

        def rows(ap, n):
            return ap[:, n * P:(n + 1) * P]

        block = ctx.enter_context(nc.Block())

        @block.sync
        def _(sp):
            def rows_of(dram, c):
                return dram[bass.ds(c, 1), :, :].rearrange("o (n p) d -> p (o n) d", p=P)

            def load_x(c, wait=True):
                if wait:
                    sp.wait_ge(norm_done[0], c)
                sp.dma_start(x_in[:, :, :], rows_of(x, c)).then_inc(x_in_done, 16)

            def load_res(c, wait=True):
                if wait:
                    sp.wait_ge(x1_done, c)
                sp.dma_start(x_res[:, :, :], rows_of(x, c)).then_inc(x_res_done, 16)

            def store(c):
                sp.wait_ge(out_done, c + 1)
                sp.dma_start(rows_of(out, c), out_sb[:, :, :]).then_inc(out_stored, 16)

            load_x(0, wait=False)
            sp.dma_start(sm_raw[:, CE:CE + E], cent_t).then_inc(small_in[0], 16)
            sp.dma_start(ident[:, :], ident_in).then_inc(small_in[0], 16)
            sp.dma_start(bias_b[:, :], ebias.partition_broadcast(P)).then_inc(small_in[0], 16)
            for i in range(NPIECE):
                js = slice(i * JP, (i + 1) * JP)
                sp.dma_start(wu_raw[:, js, :], w_up[:, js, :]).then_inc(wu_in[i], 16)
            load_x(1)
            load_res(0, wait=False)
            load_x(2)
            load_res(1)
            with sp.Fori(2, B - 1) as c:
                load_x(c + 1)
                store(c - 2)
                sp.wait_ge(out_stored, 16 * (c - 1))
                load_res(c)
            store(B - 3)
            sp.wait_ge(out_stored, 16 * (B - 2))
            load_res(B - 1)
            store(B - 2)
            store(B - 1)
            sp.wait_ge(out_stored, 16 * B)

        @block.gpsimd
        def _(pool):
            def rstd_of(k, c):
                hold(pool, mv_done[k], c + 1)
                nc.gpsimd.tensor_scalar_add(var_eps[k][:, :], mv[k][:, :, 1], LN_EPS).then_inc(eps_done[k], 1)
                pool.wait_ge(eps_done[k], c + 1)
                nc.gpsimd.tensor_tensor(rstd[k][:, :], var_eps[k][:, :], neg_half[:, :], ALU.pow).then_inc(rstd_done[k], 1)

            def spread(q, n):
                pool.wait_ge(inv_done[q], n + 1)
                nc.gpsimd.tensor_tensor(
                    w_dup[:, :, :, :], w_sel[:, :, :].unsqueeze(3).to_broadcast([P, NB, E, R]),
                    w_inv[:, :].unsqueeze(2).unsqueeze(3).to_broadcast([P, NB, E, R]), ALU.mult).then_inc(dup_done[q], 1)

            def low_part(ph, t):
                i = t % GRING
                pool.wait_ge(hi_done, NT * ph.p + t + 1)
                nc.gpsimd.tensor_tensor(g_lo[:, i, :], gated[:, t // 2 % ORING, :], g_hi[:, i, :].bitcast(fp32),
                                        ALU.subtract).then_inc(lo_done[1], 1)

            def phase(ph):
                for t in range(SLOTS):
                    if (t - 1) % 2 and 0 < t <= NT:
                        low_part(ph, t - 1)
                    for k, c in ((0, ph.norm0), (1, ph.mid), (2, ph.norm2)):
                        if ph.at.get(f"rstd{k}") == t:
                            rstd_of(k, c)
                    if ph.at.get("xu") == t:
                        pool.wait_ge(norm_done[1], ph.mid + 1)
                        nc.gpsimd.tensor_tensor(xu[:, :, :], x1[:, :, :], normed[1][:, :, :], ALU.add).then_inc(xu_done, 1)
                    if ph.at.get("gamma") == t:
                        hold(pool, tanh_done, ph.mid + 1)
                        nc.gpsimd.tensor_scalar(gamma[:, :], th[:, :], 0.5, 0.5, ALU.mult, ALU.add).then_inc(gamma_done, 1)
                    if ph.at.get("keep") == t:
                        if ph.post is not None:
                            pool.wait_ge(out_done, ph.post + 1)
                        hold(pool, x2_done, ph.keep + 1)
                        nc.gpsimd.tensor_copy(x2_kept[:, :, :], x2[:, :, :]).then_inc(kept_done, 1)
                    if ph.at.get("cw") == t:
                        spread(1 - ph.q, ph.prep[0])

            nc.gpsimd.memset(neg_half[:, :], -0.5).then_inc(power_set, 1)
            pool.wait_ge(power_set, 1)
            rstd_of(0, 0)
            rstd_of(0, 1)
            spread(0, 0)
            over_phases(pool, phase)

        @block.scalar
        def _(act):
            def x_high(q, n):
                act.wait_ge(x_turned[q], n + 1)
                nc.scalar.copy(x_hi[q][:, :], side1).then_inc(x_hi_done[q], 1)

            def sigmoid(q, n):
                act.wait_ge(aff_done[q], n + 1)
                nc.scalar.activation(sig[:, :, :], side1[:, 0:NB * E].rearrange("p (n e) -> p n e", n=NB),
                                     ACT.Sigmoid).then_inc(sig_done[q], 1)

            def cw_copy(q, n):
                act.wait_ge(cw_turned[q], n + 1)
                nc.scalar.copy(cw[q][:, :], side0).then_inc(cw_done[q], 1)

            def silu(ph, t):
                i, w = t % RING, width(t)
                act.wait_ge(up_done, NT * ph.p + t + 1)
                nc.scalar.activation(up[i][:, 0:w], up[i][:, 0:w], ACT.Silu).then_inc(silu_done, 1)

            def high_part(ph, t):
                w = width(t)
                if t < NJ:
                    act.wait_ge(gate_done, NJ * ph.p + t + 1)
                else:
                    act.wait_ge(silu_done, NT * ph.p + t + 1)
                src = gated[:, t // 2 % ORING, 0:w] if t % 2 else up[t % RING][:, 0:w]
                nc.scalar.copy(g_hi[:, t % GRING, 0:w], src).then_inc(hi_done, 1)

            def y_copy(p):
                act.wait_ge(down_done, NT * p)
                act.wait_ge(y_turned, p - 1)
                nc.scalar.copy(y_sb[:, :], y_ps[:, :]).then_inc(y_copied, 1)

            def u_high(c):
                act.wait_ge(u_turned, c + 1)
                nc.scalar.copy(u_hi[:, 1:T], side1[:, 1:T])
                nc.scalar.copy(e0_hi[:, 0:1], side1[:, 0:1])
                nc.scalar.copy(e1_hi[:, P - 1:P], side1[:, T - 1:T]).then_inc(u_hi_done, 1)

            def phase(ph):
                for t in range(SLOTS):
                    if t < NT:
                        silu(ph, t)
                    if 0 < t <= NT:
                        high_part(ph, t - 1)
                    if ph.first and t % JP == 1 and t < NJ:
                        split_high(wd_hi, wd_raw, wd_in, t // JP)
                    if ph.at.get("y") == t:
                        y_copy(ph.p)
                    if ph.at.get("x_hi") == t:
                        x_high(1 - ph.q, ph.prep[0])
                    if ph.at.get("sig") == t:
                        sigmoid(1 - ph.q, ph.prep[0])
                    if ph.at.get("cw_copy") == t:
                        cw_copy(1 - ph.q, ph.prep[0])
                    if ph.at.get("u_hi") == t:
                        u_high(ph.mid)
                    if ph.at.get("tanh") == t:
                        act.wait_ge(att_done, ph.mid + 1)
                        nc.scalar.activation(th[:, :].unsqueeze(2), att[:, :, D:D + 1], ACT.Tanh, bias=b_half[:, :],
                                             scale=0.5).then_inc(tanh_done, 1)

            def split_high(hi, raw, arrived, i):
                js = slice(i * JP, (i + 1) * JP)
                act.wait_ge(arrived[i], 16)
                nc.scalar.copy(hi[:, js, :], raw[:, js, :]).then_inc(w_hi_done, 1)

            act.dma_start(sm_raw[:, SU + F:SU + 2 * F], ws_up).then_inc(small_in[1], 16)
            act.dma_start(sm_raw[0:F, SDL:SDL + D], ws_down).then_inc(small_in[1], 16)
            act.dma_start(sm_raw[F:P, SDH:SDH + D], ws_down).then_inc(small_in[1], 16)
            act.dma_start(sm_raw[:, A1:A1 + D], wb_t).then_inc(small_in[1], 16)
            act.dma_start(sm_raw[:, A2:A2 + D], wbf_t).then_inc(small_in[1], 16)
            act.dma_start(sm_raw[:, I1:I1 + D], ident_in).then_inc(small_in[1], 16)
            act.dma_start(sm_raw[:, I2:I2 + D], ident_in).then_inc(small_in[1], 16)
            act.wait_ge(consts_set, 1)
            act.dma_start(sm_raw[:, I1 + D:I1 + D + 1], w1).then_inc(small_in[2], 16)
            act.dma_start(sm_raw[:, I2 + D:I2 + D + 1], w2).then_inc(small_in[2], 16)
            act.dma_start(wb_sb[:, :], wb).then_inc(small_in[2], 16)
            act.dma_start(wbf_sb[:, :], wbf).then_inc(small_in[2], 16)
            act.dma_start(b_col[:, :], b_in.partition_broadcast(P)).then_inc(small_in[2], 16)
            for i in range(NPIECE):
                js = slice(i * JP, (i + 1) * JP)
                act.dma_start(wd_raw[:, js, :], w_down[:, js, :]).then_inc(wd_in[i], 16)
            act.wait_ge(small_in[0], 48)
            nc.scalar.copy(sm_hi[:, CE:CE + E], sm_raw[:, CE:CE + E]).then_inc(sm_hi_done, 1)
            x_high(0, 0)
            sigmoid(0, 0)
            for i in range(NPIECE):
                split_high(wu_hi, wu_raw, wu_in, i)
            act.wait_ge(v_copied, 2)
            nc.scalar.copy(sm_hi[:, 0:CE], sm_raw[:, 0:CE])
            nc.scalar.copy(sm_hi[:, A1:SW], sm_raw[:, A1:SW]).then_inc(sm_hi_done, 1)
            cw_copy(0, 0)
            over_phases(act, phase)
            y_copy(2 * B)

        @block.vector
        def _(dve):
            def stat(k, c, blocks=range(NB), last=True):
                if k == 0:
                    dve.wait_ge(x_in_done, 16 * (c + 1))
                else:
                    dve.wait_ge(norm_from_done[k], c + 1)
                for n in blocks:
                    made = nc.vector.bn_stats(stats[k][:, n, :], norm_from[k][:, n, :])
                if last:
                    made.then_inc(stat_done[k], 1)

            def aggr(k, c):
                hold(dve, stat_done[k], c + 1)
                for n in range(NB):
                    last = nc.vector.bn_aggr(mv[k][:, n, :], stats[k][:, n, :])
                last.then_inc(mv_done[k], 1)

            def norm(k, c, blocks=range(NB), last=True):
                dve.wait_ge(rstd_done[k], c + 1)
                for n in blocks:
                    made = nc.vector.tensor_scalar(normed[k][:, n, :], norm_from[k][:, n, :], mv[k][:, n, 0:1],
                                                   rstd[k][:, n:n + 1], ALU.subtract, ALU.mult)
                if last:
                    made.then_inc(norm_done[k], 1)

            def x_low(q, n):
                dve.wait_ge(x_hi_done[q], n + 1)
                nc.vector.tensor_tensor(x_lo[q][:, :], side1, x_hi[q][:, :].bitcast(fp32), ALU.subtract).then_inc(x_lo_done[q], 1)

            def add_bias(q, n):
                dve.wait_ge(sig_done[q], n + 1)
                nc.vector.tensor_tensor(biased[:, :, :], side1[:, 0:NB * E].rearrange("p (n e) -> p n e", n=NB),
                                        bias_b[:, :].unsqueeze(1).to_broadcast([P, NB, E]), ALU.add).then_inc(bias_done[q], 1)

            def find_top(q, n):
                hold(dve, bias_done[q], n + 1)
                for m in range(NB):
                    last = nc.vector.max(top[:, m, :], biased[:, m, :])
                last.then_inc(top_done[q], 1)

            def take_top(q, n):
                hold(dve, top_done[q], n + 1)
                for m in range(NB):
                    last = nc.vector.match_replace(taken[:, m, :], top[:, m, :], biased[:, m, :], TAKEN)
                last.then_inc(taken_done[q], 1)

            def select(q, n):
                dve.wait_ge(taken_done[q], n + 1)
                nc.vector.scalar_tensor_tensor(w_sel[:, :, :], taken[:, :, :], TAKEN, sig[:, :, :],
                                               ALU.is_equal, ALU.mult).then_inc(sel_done[q], 1)

            def sum_up(q, n):
                dve.wait_ge(sel_done[q], n + 1)
                nc.vector.reduce_sum(w_sum[:, :], w_sel[:, :, :], axis=AX.X).then_inc(sum_done[q], 1)

            def add_eps(q, n):
                dve.wait_ge(sum_done[q], n + 1)
                nc.vector.tensor_scalar_add(w_eps[:, :], w_sum[:, :], SUM_EPS).then_inc(sum_eps_done[q], 1)

            def invert(q, n):
                dve.wait_ge(sum_eps_done[q], n + 1)
                nc.vector.reciprocal(w_inv[:, :], w_eps[:, :]).then_inc(inv_done[q], 1)

            def gate(ph, t):
                i = t % RING
                dve.wait_ge(silu_done, NT * ph.p + t + 1)
                nc.vector.tensor_tensor(gated[:, t // 2 % ORING, :] if t % 2 else up[i][:, :], up[i][:, :], cw[ph.q][:, :],
                                        ALU.mult).then_inc(gate_done, 1)

            def low_part(ph, t):
                i, w = t % GRING, width(t)
                dve.wait_ge(hi_done, NT * ph.p + t + 1)
                nc.vector.tensor_tensor(g_lo[:, i, 0:w], up[t % RING][:, 0:w], g_hi[:, i, 0:w].bitcast(fp32),
                                        ALU.subtract).then_inc(lo_done[0], 1)

            def split_low(lo, raw, hi, i, n):
                js = slice(i * JP, (i + 1) * JP)
                dve.wait_ge(w_hi_done, n)
                nc.vector.tensor_tensor(lo[:, js, :], raw[:, js, :], hi[:, js, :].bitcast(fp32),
                                        ALU.subtract).then_inc(w_lo_done, 1)

            def u_low(c):
                dve.wait_ge(u_hi_done, c + 1)
                for lo, hi, a, b, s in ((u_lo, u_hi, 1, T, 1), (e0_lo, e0_hi, 0, 1, 0), (e1_lo, e1_hi, P - 1, P, T - 1)):
                    last = nc.vector.tensor_tensor(lo[:, a:b], side1[:, s:s + b - a], hi[:, a:b].bitcast(fp32), ALU.subtract)
                last.then_inc(u_lo_done, 1)

            def last_sum(p, c):
                dve.wait_ge(y_turned, p)
                dve.wait_ge(kept_done, c + 1)
                nc.vector.scalar_tensor_tensor(out_sb[:, :, :], side0_rows, 0.5, x2_kept[:, :, :],
                                               ALU.mult, ALU.add).then_inc(out_done, 1)

            def phase(ph):
                q = 1 - ph.q
                n = ph.prep[0] if ph.prep else None
                for t in range(SLOTS):
                    if t == 0:
                        dve.wait_ge(cw_done[ph.q], ph.use + 1)
                    if t < NJ:
                        gate(ph, t)
                    if t % 2 and t <= NT:
                        low_part(ph, t - 1)
                    if ph.first and t % JP == 2 and t < NJ:
                        split_low(wd_lo, wd_raw, wd_hi, t // JP, NPIECE + t // JP + 1)
                    for k, c in ((0, ph.norm0), (1, ph.mid), (2, ph.norm2 if ph.norm2 is not None else ph.mid)):
                        blocks, last = halves(ph, f"stat{k}", t)
                        if blocks:
                            stat(k, c, blocks, last)
                        if ph.at.get(f"aggr{k}") == t:
                            aggr(k, c)
                        blocks, last = halves(ph, f"norm{k}", t)
                        if blocks:
                            norm(k, c, blocks, last)
                    for name, step in (("x_lo", x_low), ("bias", add_bias), ("max", find_top), ("take", take_top),
                                       ("gate", select), ("sum", sum_up), ("eps", add_eps), ("inv", invert)):
                        if ph.at.get(name) == t:
                            step(q, n)
                    if ph.at.get("x1") == t:
                        dve.wait_ge(y_turned, ph.p)
                        dve.wait_ge(x_res_done, 16 * (ph.mid + 1))
                        nc.vector.scalar_tensor_tensor(x1[:, :, :], side0_rows, 0.5, x_res[:, :, :],
                                                       ALU.mult, ALU.add).then_inc(x1_done, 1)
                    if ph.at.get("u_lo") == t:
                        u_low(ph.mid)
                    if ph.at.get("t1") == t:
                        dve.wait_ge(tanh_done, ph.mid + 1)
                        nc.vector.tensor_tensor(t1[:, :, :], att[:, :, 0:D], normed[1][:, :, :],
                                                ALU.subtract).then_inc(t1_done, 1)
                    blocks, last = halves(ph, "x2", t)
                    if blocks:
                        dve.wait_ge(t1_done, ph.mid + 1)
                        dve.wait_ge(gamma_done, ph.mid + 1)
                        dve.wait_ge(xu_done, ph.mid + 1)
                        dve.wait_ge(kept_done, ph.mid)
                        for m in blocks:
                            made = nc.vector.scalar_tensor_tensor(x2[:, m, :], t1[:, m, :], gamma[:, m:m + 1], xu[:, m, :],
                                                                  ALU.mult, ALU.add)
                        if last:
                            made.then_inc(x2_done, 1)
                    if ph.at.get("out") == t:
                        last_sum(ph.p, ph.post)

            nc.vector.memset(sm_raw[:, SU:SU + F], 0.0)
            nc.vector.memset(sm_raw[:, SU + 2 * F:SU + 3 * F], 0.0)
            nc.vector.memset(sm_raw[F:P, SDL:SDL + D], 0.0)
            nc.vector.memset(sm_raw[0:F, SDH:SDH + D], 0.0)
            nc.vector.memset(sm_raw[:, I1 + D:I1 + AW], 0.0)
            nc.vector.memset(sm_raw[:, I2 + D:I2 + AW], 0.0)
            for edge in (u_hi, u_lo):
                nc.vector.memset(edge[:, 0:1].bitcast(fp32), 0.0)
                nc.vector.memset(edge[:, T:T + 2].bitcast(fp32), 0.0)
            for edge in (e0_hi, e0_lo, e1_hi, e1_lo):
                last = nc.vector.memset(edge[:, :].bitcast(fp32), 0.0)
            last.then_inc(consts_set, 1)
            stat(0, 0)
            aggr(0, 0)
            norm(0, 0)
            stat(0, 1)
            aggr(0, 1)
            dve.wait_ge(sm_hi_done, 1)
            nc.vector.tensor_tensor(sm_lo[:, CE:CE + E], sm_raw[:, CE:CE + E], sm_hi[:, CE:CE + E].bitcast(fp32),
                                    ALU.subtract).then_inc(sm_lo_done, 1)
            x_low(0, 0)
            add_bias(0, 0)
            find_top(0, 0)
            take_top(0, 0)
            select(0, 0)
            sum_up(0, 0)
            add_eps(0, 0)
            invert(0, 0)
            dve.wait_ge(x_turned[0], 1)
            norm(0, 1)
            for i in range(NPIECE):
                split_low(wu_lo, wu_raw, wu_hi, i, i + 1)
            dve.wait_ge(small_in[2], 80)
            nc.vector.tensor_scalar_mul(b_half[:, :], b_col[:, :], 0.5).then_inc(half_b_done, 1)
            dve.wait_ge(v_done, 1)
            nc.vector.tensor_copy(sm_raw[:, A1 + D:A1 + AW], side0[:, 256:258]).then_inc(v_copied, 1)
            nc.vector.tensor_copy(sm_raw[:, A2 + D:A2 + AW], side0[:, 258:260]).then_inc(v_copied, 1)
            dve.wait_ge(sm_hi_done, 2)
            nc.vector.tensor_tensor(sm_lo[:, 0:CE], sm_raw[:, 0:CE], sm_hi[:, 0:CE].bitcast(fp32), ALU.subtract)
            nc.vector.tensor_tensor(sm_lo[:, A1:SW], sm_raw[:, A1:SW], sm_hi[:, A1:SW].bitcast(fp32),
                                    ALU.subtract).then_inc(sm_lo_done, 1)
            over_phases(dve, phase)
            dve.wait_ge(out_stored, 16 * (B - 1))
            last_sum(2 * B, B - 1)

        @block.tensor
        def _(pe):
            def split_product(o, a, b, start, stop):
                nc.tensor.matmul(o, a[0], b[0], start=start, stop=False)
                nc.tensor.matmul(o, a[0], b[1], start=False, stop=False)
                return nc.tensor.matmul(o, a[1], b[0], start=False, stop=stop)

            def small(a, b):
                return sm_hi[:, a:b], sm_lo[:, a:b]

            def turn(dst, src):
                for n in range(NB):
                    last = nc.tensor.transpose(rows(dst, n), src(n), ident[:, :])
                return last

            def turn_x(q, n, k, c):
                pe.wait_ge(norm_done[k], c + 1)
                turn(side1, lambda m: normed[k][:, m, :]).then_inc(x_turned[q], 1)

            def affinities(q, n):
                pe.wait_ge(x_lo_done[q], n + 1)
                for m in range(NB):
                    last = split_product(side1[:, m * E:(m + 1) * E], (rows(x_hi[q], m), rows(x_lo[q], m)),
                                         small(CE, CE + E), True, True)
                last.then_inc(aff_done[q], 1)

            def turn_cw(q, n):
                pe.wait_ge(dup_done[q], n + 1)
                turn(side0, lambda m: w_dup[:, m, :, :].rearrange("p e r -> p (e r)")).then_inc(cw_turned[q], 1)

            def turn_y(p):
                pe.wait_ge(y_copied, p)
                turn(side0, lambda m: rows(y_sb, m)).then_inc(y_turned, 1)

            def attention(c):
                pe.wait_ge(u_lo_done, c + 1)
                for m in range(NB):
                    o, a = att[:, m, 0:AW], m * P
                    edge = m in (0, NB - 1)
                    split_product(o, (u_hi[:, a:a + P], u_lo[:, a:a + P]), small(A1, A1 + AW), True, False)
                    last = split_product(o, (u_hi[:, a + 1:a + 1 + P], u_lo[:, a + 1:a + 1 + P]),
                                         small(A2, A2 + AW), False, not edge)
                    if m == 0:
                        last = split_product(o, (e0_hi[:, :], e0_lo[:, :]), small(I1, I1 + AW), False, True)
                    if m == NB - 1:
                        last = split_product(o, (e1_hi[:, :], e1_lo[:, :]), small(I2, I2 + AW), False, True)
                last.then_inc(att_done, 1)

            def up_product(ph, t):
                q, o = ph.q, up[t % RING]
                if t < NJ:
                    last = split_product(o[:, :], (wu_hi[:, t, :], wu_lo[:, t, :]), (x_hi[q][:, :], x_lo[q][:, :]), True, True)
                else:
                    for h in range(2):
                        s, a = SU + F * (1 - h), h * HT
                        last = split_product(o[:, 0:HT], small(s, s + P), (x_hi[q][:, a:a + HT], x_lo[q][:, a:a + HT]), h == 0, h == 1)
                last.then_inc(up_done, 1)

            def down_product(ph, t):
                made, t = low_count(ph, t), before(t)[1]
                pe.wait_ge(lo_done[t % 2], made)
                i, w = t % GRING, width(t)
                g = (g_hi[:, i, 0:w], g_lo[:, i, 0:w])
                if t < NJ:
                    last = split_product(y_ps[:, :], (wd_hi[:, t, :], wd_lo[:, t, :]), g, t == 0, False)
                else:
                    for h in range(2):
                        s, a = (SDL, SDH)[h], h * HT
                        last = split_product(y_ps[:, a:a + HT], small(s, s + D), g, False, h == 1)
                last.then_inc(down_done, 1)

            def free_bank(ph, t):
                back, tile = before(t)
                if tile % 2:
                    pe.wait_ge(gate_done, NJ * (ph.p - back) + tile + 1)
                else:
                    pe.wait_ge(lo_done[0], low_count(ph, t))

            def phase(ph):
                q = 1 - ph.q
                for t in range(SLOTS):
                    if ph.first and t % JP == LAG and t < NJ:
                        pe.wait_ge(w_lo_done, NPIECE + t // JP + 1)
                    if before(t - LAG)[1] < NT and not (ph.first and t < LAG):
                        if t == LAG:
                            pe.wait_ge(y_copied, ph.p)
                        down_product(ph, t - LAG)
                    if ph.first and t < NJ and t % JP == 0:
                        pe.wait_ge(w_lo_done, t // JP + 1)
                    if t == 0:
                        pe.wait_ge(x_lo_done[ph.q], ph.use + 1)
                    if t < NT and before(t - RING)[1] < NT and not (ph.first and t < RING):
                        free_bank(ph, t - RING)
                    if t < NT:
                        up_product(ph, t)
                    if ph.at.get("x_t") == t:
                        turn_x(q, *ph.prep)
                    if ph.at.get("aff") == t:
                        affinities(q, ph.prep[0])
                    if ph.at.get("y_t") == t:
                        if ph.steady_a:
                            pe.wait_ge(t1_done, ph.norm2 + 1)
                        else:
                            pe.wait_ge(cw_done[ph.q], ph.use + 1)
                        turn_y(ph.p)
                    if ph.at.get("cw_t") == t:
                        if ph.steady_a:
                            pe.wait_ge(out_done, ph.post + 1)
                        if ph.first:
                            pe.wait_ge(cw_done[0], 1)
                        turn_cw(q, ph.prep[0])
                    if ph.at.get("u_t") == t:
                        if ph.steady_b:
                            pe.wait_ge(bias_done[q], ph.prep[0] + 1)
                        pe.wait_ge(norm_done[1], ph.mid + 1)
                        turn(side1, lambda m: normed[1][:, m, :]).then_inc(u_turned, 1)
                    if ph.at.get("attn") == t:
                        if ph.steady_b:
                            pe.wait_ge(cw_done[q], ph.prep[0] + 1)
                        attention(ph.mid)

            pe.wait_ge(small_in[0], 48)
            turn_x(0, 0, 0, 0)
            pe.wait_ge(sm_lo_done, 1)
            affinities(0, 0)
            pe.wait_ge(small_in[2], 80)
            nc.tensor.matmul(side0[:, 256:258], wb_sb[:, :], sm_raw[:, I1 + D:I1 + AW], start=True, stop=True)
            nc.tensor.matmul(side0[:, 258:260], wbf_sb[:, :], sm_raw[:, I2 + D:I2 + AW], start=True, stop=True).then_inc(v_done, 1)
            pe.wait_ge(v_copied, 2)
            turn_cw(0, 0)
            pe.wait_ge(sm_lo_done, 2)
            over_phases(pe, phase)
            for t in range(SLOTS - LAG, NT):
                down_product(Phase(2 * B - 1, 1, {}), t)
            pe.wait_ge(out_done, B - 1)
            turn_y(2 * B)


def kernel(L0_attn_u, L0_attn_WA, L0_attn_WB, L0_attn_WAf, L0_attn_WBf, L0_attn_w1, L0_attn_w2, L0_attn_b, L0_attn_Wc,
           L0_ffn_centroids, L0_ffn_expert_biases, L0_ffn_Ws_up, L0_ffn_Ws_down, L0_ffn_W_up, L0_ffn_W_down):
    import numpy as np
    import concourse.bacc as bacc
    from concourse.bass_utils import run_bass_kernel_spmd

    def lay(a):
        return np.ascontiguousarray(a)

    WB, WBf = np.asarray(L0_attn_WB), np.asarray(L0_attn_WBf)
    w_up = np.asarray(L0_ffn_W_up).reshape(E, D, NJ, R).transpose(1, 2, 0, 3).reshape(D, NJ, P)
    w_down = np.asarray(L0_ffn_W_down).reshape(E, NJ, R, D).transpose(0, 2, 1, 3).reshape(P, NJ, D)
    arrays = {
        "x": lay(L0_attn_u), "ident": np.eye(P, dtype=np.float32), "cent_t": lay(np.asarray(L0_ffn_centroids).T),
        "ebias": lay(L0_ffn_expert_biases), "ws_up": lay(L0_ffn_Ws_up), "ws_down": lay(L0_ffn_Ws_down),
        "w_up": lay(w_up), "w_down": lay(w_down), "wb": lay(WB), "wb_t": lay(WB.T), "wbf": lay(WBf), "wbf_t": lay(WBf.T),
        "w1": lay(np.asarray(L0_attn_w1).reshape(D, 1)), "w2": lay(np.asarray(L0_attn_w2).reshape(D, 1)),
        "b": lay(L0_attn_b),
    }
    nc = bacc.Bacc("TRN2", target_bir_lowering=False, num_devices=1)
    args = [nc.dram_tensor(f"in_{k}", a.shape, mybir.dt.from_np(a.dtype), kind="ExternalInput").ap() for k, a in arrays.items()]
    out = nc.dram_tensor("out_0", (B, T, D), mybir.dt.float32, kind="ExternalOutput").ap()
    build(nc, *args, out)
    r = run_bass_kernel_spmd(nc, [{f"in_{k}": a for k, a in arrays.items()}], core_ids=[0])
    return r.results[0]["out_0"]
```

```python
from contextlib import ExitStack

import concourse.bass as bass
from concourse import mybir

B, T, D = 8, 512, 128
E, F, TOPK = 64, 64, 8
P = 128
NB = T // P
R = P // E
NJ = F // R
NT = NJ + 1
HT = T // 2
RING = 5
SLOTS = -(-NT // RING) * RING
LAG = RING + 1
GRING = LAG + 1
ORING = 4
NLOW = (NT // 2 + 1, NT // 2)
AW = D + 2
AS = 256
NPIECE = 4
JP = NJ // NPIECE
LN_EPS = 1e-5
WARM_START, WARM_ROWS, WARM_ROUTE, WARM_LATE = 13, 4, 8, 9
SUM_EPS = 1e-8
TAKEN = -3.0e38


class Phase:

    def __init__(self, p, q, at, prep=None, norm0=None, mid=None, norm2=None, keep=None, post=None, first=False, use=None, late=False):
        self.p, self.q, self.at, self.first, self.late = p, q, at, first, late
        self.use = p // 2 if isinstance(p, int) else use
        self.steady_a, self.steady_b = prep is not None and post is not None, prep is not None and mid is not None and norm2 is None
        self.prep, self.norm0, self.mid, self.norm2, self.keep, self.post = prep, norm0, mid, norm2, keep, post


PREP = ("x_t", "x_hi", "x_lo", "aff", "sig", "bias", "max", "take", "gate", "sum", "eps", "inv", "cw", "cw_t", "cw_copy")
MID = ("y_t", "x1", "stat1", "aggr1", "rstd1", "norm1", "xu", "u_t", "u_hi", "u_lo",
       "attn", "tanh", "gamma", "t1", "x2")
NORM0, NORM2 = ("stat0", "aggr0", "rstd0", "norm0"), ("stat2", "aggr2", "rstd2", "norm2")


def places(names, at):
    return dict(zip(names, at))


LATE = 3
AT_FIRST = {
    "norm0": (4, 6), **places(PREP, (9, 10, 11, 14, 15, 16, 17, 19, 21, 23, 25, 26, 27, 31, 32)),
    "v": 12, "v_copy": 14, "sm_hi": 19, "sm_lo": (23, 26),
    "wu_hi": (None, None, 5, 13), "wu_lo": (None, None, 6, 14),
    "wd_hi": (None, 8, 15, 22), "wd_lo": (None, 9, 16, 24),
}
AT_MID_PREP = {
    "y": 2,
    **places(MID, (5, 6, (7, 7), 8, 8, (9, 10), 12, 14, 14, 13, 17, 18, 18, 17, (19, 19))),
    **places(NORM2, ((20, 20), 21, 22, (23, 23))),
    **places(PREP[:-2], (27, 28, 27, 31, 32, 31, 31, 32, 32, 33, 33, 33, 33)),
}
AT_SECOND = {**AT_MID_PREP, "keep": 24, **places(NORM0, ((0, 2), 3, 3, (4, 5)))}
AT_STEADY_A = {
    "y": 2, "y_t": 6, "out": 8, **places(NORM2[1:], (0, 1, (2, 4))),
    **places(PREP, (7, 8, 10, 13, 14, 16, 18, 20, 22, 24, 26, 27, 28, 31, 32)),
    "keep": 11, **places(NORM0, ((12, 14), 16, 17, (28, 30))),
}
AT_STEADY_B = {
    "y": 2,
    **places(PREP, (1, 2, 4, 8, 9, 10, 14, 15, 17, 19, 20, 21, 22, 26, 26)),
    **places(MID, (6, 8, (10, 12), 13, 14, (16, 18), 19, 22, 23, 24, 28, 29, 30, 30, (32, 33))),
    "stat2": (34, 34),
}
AT_THIRD = {**{k: v for k, v in AT_STEADY_B.items() if k != "y"}, **places(PREP[:6], (4, 5, 6, 9, 10, 11))}
AT_LAST = {"y_t": 6, "out": 8, "keep": 9}


def over_phases(eng, phase):
    phase(Phase(0, 0, AT_FIRST, prep=(0, 0, 1), norm0=1, first=True, late=True))
    phase(Phase(1, 1, AT_SECOND, mid=0, norm2=0, prep=(1, 2, 0), keep=0, norm0=2))
    phase(Phase(2, 0, AT_THIRD, prep=(1, 0, 2), mid=1, late=True))
    with eng.Fori(2, B - 1) as c:
        phase(Phase(2 * c - 1, 1, AT_STEADY_A, norm2=c - 1, post=c - 2, prep=(c, 2, c - 1), keep=c - 1, norm0=c + 1, use=c - 1))
        phase(Phase(2 * c, 0, AT_STEADY_B, prep=(c, 0, c + 1), mid=c, use=c))
    c = B - 1
    at = {k: v for k, v in AT_STEADY_A.items() if k not in NORM0}
    phase(Phase(2 * c - 1, 1, at, norm2=c - 1, post=c - 2, prep=(c, 2, c - 1), keep=c - 1))
    phase(Phase(2 * c, 0, AT_MID_PREP, mid=c, norm2=c, prep=(c, 2, c)))
    phase(Phase(2 * c + 1, 1, AT_LAST, post=c - 1, keep=c, late=True))


def build(nc, x, ident_in, cent_t, ebias, ws_up, ws_down, w_up, w_down, wb, wb_t, wbf, wbf_t, w1, w2, b_in, out):
    fp32, fp32r = mybir.dt.float32, mybir.dt.float32r
    ALU, ACT, AX = mybir.AluOpType, mybir.ActivationFunctionType, mybir.AxisListType
    ctx = ExitStack()
    with ctx:
        def sb(name, shape, dt=fp32):
            return ctx.enter_context(nc.sbuf_tensor(name, shape, dt))

        def sem(name):
            return ctx.enter_context(nc.semaphore(name))

        wu_raw, wd_raw = sb("wu_raw", [P, NJ, P]), sb("wd_raw", [P, NJ, P])
        wu_hi, wu_lo = sb("wu_hi", [P, NJ, P], fp32r), sb("wu_lo", [P, NJ, P], fp32r)
        wd_hi, wd_lo = sb("wd_hi", [P, NJ, P], fp32r), sb("wd_lo", [P, NJ, P], fp32r)
        SU, SDL, SDH = 0, 3 * F, 3 * F + D
        CE = SDH + D
        A1, A2 = CE + E, CE + E + AW
        I1, I2 = A2 + AW, A2 + 2 * AW
        SW = I2 + AW
        sm_raw = sb("sm_raw", [P, SW])
        sm_hi, sm_lo = sb("sm_hi", [P, SW], fp32r), sb("sm_lo", [P, SW], fp32r)
        wb_sb, wbf_sb = sb("wb_sb", [P, P]), sb("wbf_sb", [P, P])
        ident = sb("ident", [P, P])
        bias_b = sb("bias_b", [P, E])
        b_col, b_half = sb("b_col", [P, 1]), sb("b_half", [P, 1])
        neg_half = sb("neg_half", [P, NB])

        x_hi = [sb(f"x_hi{q}", [P, T], fp32r) for q in range(2)]
        x_lo = [sb(f"x_lo{q}", [P, T], fp32r) for q in range(2)]
        cw = [sb(f"cw{q}", [P, T]) for q in range(2)]
        gated = sb("gated", [P, ORING, T])
        g_hi, g_lo = sb("g_hi", [P, GRING, T], fp32r), sb("g_lo", [P, GRING, T], fp32r)

        x_in, x_res = sb("x_in", [P, NB, D]), sb("x_res", [P, NB, D])
        x1, x2, x2_kept = sb("x1", [P, NB, D]), sb("x2", [P, NB, D]), sb("x2_kept", [P, NB, D])
        out_sb = sb("out_sb", [P, NB, D])
        normed = [sb(f"normed{k}", [P, NB, D]) for k in range(3)]
        xu, t1 = sb("xu", [P, NB, D]), sb("t1", [P, NB, D])
        y_sb = sb("y_sb", [P, T])
        stats = [sb(f"stats{k}", [P, NB, 6]) for k in range(3)]
        mv = [sb(f"mv{k}", [P, NB, 2]) for k in range(3)]
        var_eps = [sb(f"var_eps{k}", [P, NB]) for k in range(3)]
        rstd = [sb(f"rstd{k}", [P, NB]) for k in range(3)]
        th, gamma = sb("th", [P, NB]), sb("gamma", [P, NB])
        u_hi, u_lo = sb("u_hi", [P, T + 2], fp32r), sb("u_lo", [P, T + 2], fp32r)
        e0_hi, e0_lo = sb("e0_hi", [P, P], fp32r), sb("e0_lo", [P, P], fp32r)
        e1_hi, e1_lo = sb("e1_hi", [P, P], fp32r), sb("e1_lo", [P, P], fp32r)
        sig, biased, taken = sb("sig", [P, NB, E]), sb("biased", [P, NB, E]), sb("taken", [P, NB, E])
        top = sb("top", [P, NB, TOPK])
        w_sel, w_dup = sb("w_sel", [P, NB, E]), sb("w_dup", [P, NB, E, R])
        w_sum, w_eps, w_inv = sb("w_sum", [P, NB]), sb("w_eps", [P, NB]), sb("w_inv", [P, NB])

        up = [ctx.enter_context(nc.psum_tensor(f"up{i}", [P, T], fp32)) for i in range(RING)]
        y_ps = ctx.enter_context(nc.psum_tensor("y_ps", [P, T], fp32))
        side = ctx.enter_context(nc.psum_tensor("side", [P, 2 * T], fp32))
        side0, side1 = side[:, 0:T], side[:, T:2 * T]
        att = side[:, :].rearrange("p (n c) -> p n c", c=AS)
        side0_rows = side0.rearrange("p (n d) -> p n d", n=NB)

        small_in = [sem(f"small_in{i}") for i in range(3)]
        wu_in, wd_in = [sem(f"wu_in{i}") for i in range(NPIECE)], [sem(f"wd_in{i}") for i in range(NPIECE)]
        consts_set, v_done, sm_hi_done, sm_lo_done = (sem(s) for s in ("consts_set", "v_done", "sm_hi_done", "sm_lo_done"))
        v_copied, half_b_done = sem("v_copied"), sem("half_b_done")
        wu_hi_done, wd_hi_done, wd_lo_done = sem("wu_hi_done"), sem("wd_hi_done"), sem("wd_lo_done")
        wu_lo_done = [sem("wu_lo_done_vector"), sem("wu_lo_done_pool")]
        up_done, silu_done, gate_done, hi_done = (sem(s) for s in ("up_done", "silu_done", "gate_done", "hi_done"))
        lo_done = [sem("lo_done_vector"), sem("lo_done_pool")]
        down_done, y_copied, y_turned = sem("down_done"), sem("y_copied"), sem("y_turned")
        x_in_done, x_res_done, out_stored = sem("x_in_done"), sem("x_res_done"), sem("out_stored")
        stat_done, mv_done = [sem(f"stat_done{k}") for k in range(3)], [sem(f"mv_done{k}") for k in range(3)]
        eps_done, rstd_done = [sem(f"eps_done{k}") for k in range(3)], [sem(f"rstd_done{k}") for k in range(3)]
        norm_done = [sem(f"norm_done{k}") for k in range(3)]

        def pair(name):
            return [sem(f"{name}{q}") for q in range(2)]

        x_turned, x_hi_done, x_lo_done, aff_done = pair("x_turned"), pair("x_hi_done"), pair("x_lo_done"), pair("aff_done")
        sig_done, bias_done, top_done, taken_done = pair("sig_done"), pair("bias_done"), pair("top_done"), pair("taken_done")
        sel_done, sum_done, sum_eps_done, inv_done = pair("sel_done"), pair("sum_done"), pair("sum_eps_done"), pair("inv_done")
        dup_done, cw_turned, cw_done = pair("dup_done"), pair("cw_turned"), pair("cw_done")
        x1_done, xu_done, u_turned, u_hi_done, u_lo_done = (sem(s) for s in ("x1_done", "xu_done", "u_turned", "u_hi_done", "u_lo_done"))
        att_done, tanh_done, gamma_done, t1_done = (sem(s) for s in ("att_done", "tanh_done", "gamma_done", "t1_done"))
        x2_done, kept_done, out_done = sem("x2_done"), sem("kept_done"), sem("out_done")

        held, power_set = sem("held"), sem("power_set")

        norm_from = [x_in, x1, x2]
        norm_from_done = [None, x1_done, x2_done]

        def before(t):
            return (0, t) if t >= 0 else (1, t + SLOTS)

        def low_count(ph, t):
            back, t = before(t)
            return NLOW[t % 2] * (ph.p - back) + t // 2 + 1

        def halves(ph, name, t):
            at = ph.at.get(name, ())
            blocks = [n for h, a in enumerate(at) if a == t for n in range(h * NB // 2, (h + 1) * NB // 2)]
            return blocks, bool(blocks) and blocks[-1] == NB - 1

        def width(t):
            return T if t < NJ else HT

        def hold(eng, s, value):
            eng.wait_ge(s, value)
            eng.sem_inc(held, 1)

        def rows(ap, n):
            return ap[:, n * P:(n + 1) * P]

        block = ctx.enter_context(nc.Block())

        @block.sync
        def _(sp):
            def rows_of(dram, c):
                return dram[bass.ds(c, 1), :, :].rearrange("o (n p) d -> p (o n) d", p=P)

            def load_x(c, wait=True):
                if wait:
                    sp.wait_ge(norm_done[0], c)
                sp.dma_start(x_in[:, :, :], rows_of(x, c)).then_inc(x_in_done, 16)

            def load_res(c, wait=True):
                if wait:
                    sp.wait_ge(x1_done, c)
                sp.dma_start(x_res[:, :, :], rows_of(x, c)).then_inc(x_res_done, 16)

            def store(c):
                sp.wait_ge(out_done, c + 1)
                sp.dma_start(rows_of(out, c), out_sb[:, :, :]).then_inc(out_stored, 16)

            def load_pieces(i):
                js = slice(i * JP, (i + 1) * JP)
                sp.dma_start(wu_raw[:, js, :], w_up[:, js, :]).then_inc(wu_in[i], 16)
                sp.dma_start(wd_raw[:, js, :], w_down[:, js, :]).then_inc(wd_in[i], 16)

            load_x(0, wait=False)
            sp.dma_start(sm_raw[:, CE:CE + E], cent_t).then_inc(small_in[0], 16)
            sp.dma_start(ident[:, :], ident_in).then_inc(small_in[0], 16)
            sp.dma_start(bias_b[:, :], ebias.partition_broadcast(P)).then_inc(small_in[0], 16)
            load_pieces(0)
            load_pieces(1)
            load_x(1)
            sp.dma_start(wb_sb[:, :], wb).then_inc(small_in[2], 16)
            sp.dma_start(wbf_sb[:, :], wbf).then_inc(small_in[2], 16)
            sp.dma_start(b_col[:, :], b_in.partition_broadcast(P)).then_inc(small_in[2], 16)
            sp.wait_ge(consts_set, 1)
            sp.dma_start(sm_raw[:, I1 + D:I1 + D + 1], w1).then_inc(small_in[2], 16)
            sp.dma_start(sm_raw[:, I2 + D:I2 + D + 1], w2).then_inc(small_in[2], 16)
            load_pieces(2)
            sp.dma_start(sm_raw[:, SU + F:SU + 2 * F], ws_up).then_inc(small_in[1], 16)
            sp.dma_start(sm_raw[0:F, SDL:SDL + D], ws_down).then_inc(small_in[1], 16)
            sp.dma_start(sm_raw[F:P, SDH:SDH + D], ws_down).then_inc(small_in[1], 16)
            sp.dma_start(sm_raw[:, A1:A1 + D], wb_t).then_inc(small_in[1], 16)
            sp.dma_start(sm_raw[:, A2:A2 + D], wbf_t).then_inc(small_in[1], 16)
            sp.dma_start(sm_raw[:, I1:I1 + D], ident_in).then_inc(small_in[1], 16)
            sp.dma_start(sm_raw[:, I2:I2 + D], ident_in).then_inc(small_in[1], 16)
            load_pieces(3)
            load_res(0, wait=False)
            load_x(2)
            load_res(1)
            with sp.Fori(2, B - 1) as c:
                load_x(c + 1)
                store(c - 2)
                sp.wait_ge(out_stored, 16 * (c - 1))
                load_res(c)
            store(B - 3)
            sp.wait_ge(out_stored, 16 * (B - 2))
            load_res(B - 1)
            store(B - 2)
            store(B - 1)
            sp.wait_ge(out_stored, 16 * B)

        @block.gpsimd
        def _(pool):
            def rstd_of(k, c):
                hold(pool, mv_done[k], c + 1)
                nc.gpsimd.tensor_scalar_add(var_eps[k][:, :], mv[k][:, :, 1], LN_EPS).then_inc(eps_done[k], 1)
                pool.wait_ge(eps_done[k], c + 1)
                nc.gpsimd.tensor_tensor(rstd[k][:, :], var_eps[k][:, :], neg_half[:, :], ALU.pow).then_inc(rstd_done[k], 1)

            def spread(q, n):
                pool.wait_ge(inv_done[q], n + 1)
                nc.gpsimd.tensor_tensor(
                    w_dup[:, :, :, :], w_sel[:, :, :].unsqueeze(3).to_broadcast([P, NB, E, R]),
                    w_inv[:, :].unsqueeze(2).unsqueeze(3).to_broadcast([P, NB, E, R]), ALU.mult).then_inc(dup_done[q], 1)

            def low_part(ph, t):
                i = t % GRING
                pool.wait_ge(hi_done, NT * ph.p + t + 1)
                nc.gpsimd.tensor_tensor(g_lo[:, i, :], gated[:, t // 2 % ORING, :], g_hi[:, i, :].bitcast(fp32),
                                        ALU.subtract).then_inc(lo_done[1], 1)

            def split_up(i):
                js = slice(i * JP, (i + 1) * JP)
                pool.wait_ge(wu_hi_done, i + 1)
                nc.gpsimd.tensor_tensor(wu_lo[:, js, :], wu_raw[:, js, :], wu_hi[:, js, :].bitcast(fp32),
                                        ALU.subtract).then_inc(wu_lo_done[1], 1)

            def phase(ph):
                for t in range(SLOTS):
                    if (t - 1) % 2 and 0 < t <= NT:
                        low_part(ph, t - 1)
                    if t in ph.at.get("wu_lo", ()):
                        split_up(ph.at["wu_lo"].index(t))
                    for k, c in ((0, ph.norm0), (1, ph.mid), (2, ph.norm2)):
                        if ph.at.get(f"rstd{k}") == t:
                            rstd_of(k, c)
                    if ph.at.get("xu") == t:
                        pool.wait_ge(norm_done[1], ph.mid + 1)
                        nc.gpsimd.tensor_tensor(xu[:, :, :], x1[:, :, :], normed[1][:, :, :], ALU.add).then_inc(xu_done, 1)
                    if ph.at.get("gamma") == t:
                        hold(pool, tanh_done, ph.mid + 1)
                        nc.gpsimd.tensor_scalar(gamma[:, :], th[:, :], 0.5, 0.5, ALU.mult, ALU.add).then_inc(gamma_done, 1)
                    if ph.at.get("keep") == t:
                        if ph.post is not None:
                            pool.wait_ge(out_done, ph.post + 1)
                        hold(pool, x2_done, ph.keep + 1)
                        nc.gpsimd.tensor_copy(x2_kept[:, :, :], x2[:, :, :]).then_inc(kept_done, 1)
                    if ph.at.get("cw") == t:
                        spread(1 - ph.q, ph.prep[0])

            nc.gpsimd.memset(neg_half[:, :], -0.5).then_inc(power_set, 1)
            pool.wait_ge(power_set, 1)
            rstd_of(0, 0)
            split_up(1)
            spread(0, 0)
            rstd_of(0, 1)
            over_phases(pool, phase)

        @block.scalar
        def _(act):
            def x_high(q, n):
                act.wait_ge(x_turned[q], n + 1)
                nc.scalar.copy(x_hi[q][:, :], side1).then_inc(x_hi_done[q], 1)

            def sigmoid(q, n):
                act.wait_ge(aff_done[q], n + 1)
                nc.scalar.activation(sig[:, :, :], side1[:, 0:NB * E].rearrange("p (n e) -> p n e", n=NB),
                                     ACT.Sigmoid).then_inc(sig_done[q], 1)

            def cw_copy(q, n):
                act.wait_ge(cw_turned[q], n + 1)
                nc.scalar.copy(cw[q][:, :], side0).then_inc(cw_done[q], 1)

            def silu(ph, t):
                i, w = t % RING, width(t)
                act.wait_ge(up_done, NT * ph.p + t + 1)
                nc.scalar.activation(up[i][:, 0:w], up[i][:, 0:w], ACT.Silu).then_inc(silu_done, 1)

            def high_part(ph, t):
                w = width(t)
                if t < NJ:
                    act.wait_ge(gate_done, NJ * ph.p + t + 1)
                else:
                    act.wait_ge(silu_done, NT * ph.p + t + 1)
                src = gated[:, t // 2 % ORING, 0:w] if t % 2 else up[t % RING][:, 0:w]
                nc.scalar.copy(g_hi[:, t % GRING, 0:w], src).then_inc(hi_done, 1)

            def y_copy(p):
                act.wait_ge(down_done, NT * p)
                act.wait_ge(y_turned, p - 1)
                nc.scalar.copy(y_sb[:, :], y_ps[:, :]).then_inc(y_copied, 1)

            def u_high(c):
                act.wait_ge(u_turned, c + 1)
                nc.scalar.copy(u_hi[:, 1:T], side1[:, 1:T])
                nc.scalar.copy(e0_hi[:, 0:1], side1[:, 0:1])
                nc.scalar.copy(e1_hi[:, P - 1:P], side1[:, T - 1:T]).then_inc(u_hi_done, 1)

            def phase(ph):
                if ph.late:
                    for t in range(LATE + 1):
                        silu(ph, t)
                    cw_copy(ph.q, ph.use)
                    if not ph.first:
                        y_copy(ph.p)
                for t in range(SLOTS):
                    if (LATE if ph.late else -1) < t < NT:
                        silu(ph, t)
                    if 0 < t <= NT:
                        high_part(ph, t - 1)
                    if t in ph.at.get("wu_hi", ()):
                        split_up(ph.at["wu_hi"].index(t))
                    if t in ph.at.get("wd_hi", ()):
                        split_down(ph.at["wd_hi"].index(t))
                    if ph.at.get("sm_hi") == t:
                        act.wait_ge(small_in[1], 112)
                        act.wait_ge(v_copied, 2)
                        nc.scalar.copy(sm_hi[:, 0:CE], sm_raw[:, 0:CE])
                        nc.scalar.copy(sm_hi[:, A1:SW], sm_raw[:, A1:SW]).then_inc(sm_hi_done, 1)
                    if ph.at.get("y") == t:
                        y_copy(ph.p)
                    if ph.at.get("x_hi") == t:
                        x_high(1 - ph.q, ph.prep[0])
                    if ph.at.get("sig") == t:
                        sigmoid(1 - ph.q, ph.prep[0])
                    if ph.at.get("cw_copy") == t:
                        cw_copy(1 - ph.q, ph.prep[0])
                    if ph.at.get("u_hi") == t:
                        u_high(ph.mid)
                    if ph.at.get("tanh") == t:
                        act.wait_ge(att_done, ph.mid + 1)
                        nc.scalar.activation(th[:, :].unsqueeze(2), att[:, :, D:D + 1], ACT.Tanh, bias=b_half[:, :],
                                             scale=0.5).then_inc(tanh_done, 1)

            def split_up(i):
                js = slice(i * JP, (i + 1) * JP)
                act.wait_ge(wu_in[i], 16)
                nc.scalar.copy(wu_hi[:, js, :], wu_raw[:, js, :]).then_inc(wu_hi_done, 1)

            def split_down(i):
                js = slice(i * JP, (i + 1) * JP)
                act.wait_ge(wd_in[i], 16)
                nc.scalar.copy(wd_hi[:, js, :], wd_raw[:, js, :]).then_inc(wd_hi_done, 1)

            act.wait_ge(power_set, 1)
            nc.scalar.activation(th[:, :], neg_half[:, :], ACT.Sigmoid)
            act.wait_ge(small_in[0], 48)
            nc.scalar.copy(sm_hi[:, CE:CE + E], sm_raw[:, CE:CE + E]).then_inc(sm_hi_done, 1)
            split_up(0)
            x_high(0, 0)
            split_down(0)
            sigmoid(0, 0)
            split_up(1)
            over_phases(act, phase)
            y_copy(2 * B)

        @block.vector
        def _(dve):
            def stat(k, c, blocks=range(NB), last=True):
                if k == 0:
                    dve.wait_ge(x_in_done, 16 * (c + 1))
                else:
                    dve.wait_ge(norm_from_done[k], c + 1)
                for n in blocks:
                    made = nc.vector.bn_stats(stats[k][:, n, :], norm_from[k][:, n, :])
                if last:
                    made.then_inc(stat_done[k], 1)

            def aggr(k, c):
                hold(dve, stat_done[k], c + 1)
                for n in range(NB):
                    last = nc.vector.bn_aggr(mv[k][:, n, :], stats[k][:, n, :])
                last.then_inc(mv_done[k], 1)

            def norm(k, c, blocks=range(NB), last=True):
                dve.wait_ge(rstd_done[k], c + 1)
                for n in blocks:
                    made = nc.vector.tensor_scalar(normed[k][:, n, :], norm_from[k][:, n, :], mv[k][:, n, 0:1],
                                                   rstd[k][:, n:n + 1], ALU.subtract, ALU.mult)
                if last:
                    made.then_inc(norm_done[k], 1)

            def x_low(q, n):
                dve.wait_ge(x_hi_done[q], n + 1)
                nc.vector.tensor_tensor(x_lo[q][:, :], side1, x_hi[q][:, :].bitcast(fp32), ALU.subtract).then_inc(x_lo_done[q], 1)

            def add_bias(q, n):
                dve.wait_ge(sig_done[q], n + 1)
                nc.vector.tensor_tensor(biased[:, :, :], side1[:, 0:NB * E].rearrange("p (n e) -> p n e", n=NB),
                                        bias_b[:, :].unsqueeze(1).to_broadcast([P, NB, E]), ALU.add).then_inc(bias_done[q], 1)

            def find_top(q, n):
                hold(dve, bias_done[q], n + 1)
                for m in range(NB):
                    last = nc.vector.max(top[:, m, :], biased[:, m, :])
                last.then_inc(top_done[q], 1)

            def take_top(q, n):
                hold(dve, top_done[q], n + 1)
                for m in range(NB):
                    last = nc.vector.match_replace(taken[:, m, :], top[:, m, :], biased[:, m, :], TAKEN)
                last.then_inc(taken_done[q], 1)

            def select(q, n):
                dve.wait_ge(taken_done[q], n + 1)
                nc.vector.scalar_tensor_tensor(w_sel[:, :, :], taken[:, :, :], TAKEN, sig[:, :, :],
                                               ALU.is_equal, ALU.mult).then_inc(sel_done[q], 1)

            def sum_up(q, n):
                dve.wait_ge(sel_done[q], n + 1)
                nc.vector.reduce_sum(w_sum[:, :], w_sel[:, :, :], axis=AX.X).then_inc(sum_done[q], 1)

            def add_eps(q, n):
                dve.wait_ge(sum_done[q], n + 1)
                nc.vector.tensor_scalar_add(w_eps[:, :], w_sum[:, :], SUM_EPS).then_inc(sum_eps_done[q], 1)

            def invert(q, n):
                dve.wait_ge(sum_eps_done[q], n + 1)
                nc.vector.reciprocal(w_inv[:, :], w_eps[:, :]).then_inc(inv_done[q], 1)

            def gate(ph, t):
                i = t % RING
                dve.wait_ge(silu_done, NT * ph.p + t + 1)
                nc.vector.tensor_tensor(gated[:, t // 2 % ORING, :] if t % 2 else up[i][:, :], up[i][:, :], cw[ph.q][:, :],
                                        ALU.mult).then_inc(gate_done, 1)

            def low_part(ph, t):
                i, w = t % GRING, width(t)
                dve.wait_ge(hi_done, NT * ph.p + t + 1)
                nc.vector.tensor_tensor(g_lo[:, i, 0:w], up[t % RING][:, 0:w], g_hi[:, i, 0:w].bitcast(fp32),
                                        ALU.subtract).then_inc(lo_done[0], 1)

            def split_low(lo, raw, hi, i, made, done):
                js = slice(i * JP, (i + 1) * JP)
                dve.wait_ge(made, i + 1)
                nc.vector.tensor_tensor(lo[:, js, :], raw[:, js, :], hi[:, js, :].bitcast(fp32),
                                        ALU.subtract).then_inc(done, 1)

            def u_low(c):
                dve.wait_ge(u_hi_done, c + 1)
                for lo, hi, a, b, s in ((u_lo, u_hi, 1, T, 1), (e0_lo, e0_hi, 0, 1, 0), (e1_lo, e1_hi, P - 1, P, T - 1)):
                    last = nc.vector.tensor_tensor(lo[:, a:b], side1[:, s:s + b - a], hi[:, a:b].bitcast(fp32), ALU.subtract)
                last.then_inc(u_lo_done, 1)

            def last_sum(p, c):
                dve.wait_ge(y_turned, p)
                dve.wait_ge(kept_done, c + 1)
                nc.vector.scalar_tensor_tensor(out_sb[:, :, :], side0_rows, 0.5, x2_kept[:, :, :],
                                               ALU.mult, ALU.add).then_inc(out_done, 1)

            def phase(ph):
                q = 1 - ph.q
                n = ph.prep[0] if ph.prep else None
                for t in range(SLOTS):
                    if t == 0:
                        dve.wait_ge(cw_done[ph.q], ph.use + 1)
                    if t < NJ:
                        gate(ph, t)
                    if t % 2 and t <= NT:
                        low_part(ph, t - 1)
                    if t in ph.at.get("wd_lo", ()):
                        split_low(wd_lo, wd_raw, wd_hi, ph.at["wd_lo"].index(t), wd_hi_done, wd_lo_done)
                    if ph.at.get("v_copy") == t:
                        dve.wait_ge(small_in[2], 80)
                        nc.vector.tensor_scalar_mul(b_half[:, :], b_col[:, :], 0.5).then_inc(half_b_done, 1)
                        dve.wait_ge(v_done, 1)
                        nc.vector.tensor_copy(sm_raw[:, A1 + D:A1 + AW], side0[:, 256:258]).then_inc(v_copied, 1)
                        nc.vector.tensor_copy(sm_raw[:, A2 + D:A2 + AW], side0[:, 258:260]).then_inc(v_copied, 1)
                    if t in ph.at.get("sm_lo", ()):
                        a, b = ((0, CE), (A1, SW))[ph.at["sm_lo"].index(t)]
                        dve.wait_ge(sm_hi_done, 2)
                        nc.vector.tensor_tensor(sm_lo[:, a:b], sm_raw[:, a:b], sm_hi[:, a:b].bitcast(fp32),
                                                ALU.subtract).then_inc(sm_lo_done, 1)
                    for k, c in ((0, ph.norm0), (1, ph.mid), (2, ph.norm2 if ph.norm2 is not None else ph.mid)):
                        blocks, last = halves(ph, f"stat{k}", t)
                        if blocks:
                            stat(k, c, blocks, last)
                        if ph.at.get(f"aggr{k}") == t:
                            aggr(k, c)
                        blocks, last = halves(ph, f"norm{k}", t)
                        if blocks:
                            norm(k, c, blocks, last)
                    for name, step in (("x_lo", x_low), ("bias", add_bias), ("max", find_top), ("take", take_top),
                                       ("gate", select), ("sum", sum_up), ("eps", add_eps), ("inv", invert)):
                        if ph.at.get(name) == t:
                            step(q, n)
                    if ph.at.get("x1") == t:
                        dve.wait_ge(y_turned, ph.p)
                        dve.wait_ge(x_res_done, 16 * (ph.mid + 1))
                        nc.vector.scalar_tensor_tensor(x1[:, :, :], side0_rows, 0.5, x_res[:, :, :],
                                                       ALU.mult, ALU.add).then_inc(x1_done, 1)
                    if ph.at.get("u_lo") == t:
                        u_low(ph.mid)
                    if ph.at.get("t1") == t:
                        dve.wait_ge(tanh_done, ph.mid + 1)
                        nc.vector.tensor_tensor(t1[:, :, :], att[:, :, 0:D], normed[1][:, :, :],
                                                ALU.subtract).then_inc(t1_done, 1)
                    blocks, last = halves(ph, "x2", t)
                    if blocks:
                        dve.wait_ge(t1_done, ph.mid + 1)
                        dve.wait_ge(gamma_done, ph.mid + 1)
                        dve.wait_ge(xu_done, ph.mid + 1)
                        dve.wait_ge(kept_done, ph.mid)
                        for m in blocks:
                            made = nc.vector.scalar_tensor_tensor(x2[:, m, :], t1[:, m, :], gamma[:, m:m + 1], xu[:, m, :],
                                                                  ALU.mult, ALU.add)
                        if last:
                            made.then_inc(x2_done, 1)
                    if ph.at.get("out") == t:
                        last_sum(ph.p, ph.post)

            nc.vector.memset(sm_raw[:, SU:SU + F], 0.0)
            nc.vector.memset(sm_raw[:, SU + 2 * F:SU + 3 * F], 0.0)
            nc.vector.memset(sm_raw[F:P, SDL:SDL + D], 0.0)
            nc.vector.memset(sm_raw[0:F, SDH:SDH + D], 0.0)
            nc.vector.memset(sm_raw[:, I1 + D:I1 + AW], 0.0)
            nc.vector.memset(sm_raw[:, I2 + D:I2 + AW], 0.0)
            for edge in (u_hi, u_lo):
                nc.vector.memset(edge[:, 0:1].bitcast(fp32), 0.0)
                nc.vector.memset(edge[:, T:T + 2].bitcast(fp32), 0.0)
            nc.vector.memset(g_hi[:, 0, :].bitcast(fp32), 0.0)
            for edge in (e0_hi, e0_lo, e1_hi, e1_lo):
                last = nc.vector.memset(edge[:, :].bitcast(fp32), 0.0)
            last.then_inc(consts_set, 1)
            stat(0, 0)
            aggr(0, 0)
            norm(0, 0)
            dve.wait_ge(sm_hi_done, 1)
            nc.vector.tensor_tensor(sm_lo[:, CE:CE + E], sm_raw[:, CE:CE + E], sm_hi[:, CE:CE + E].bitcast(fp32),
                                    ALU.subtract).then_inc(sm_lo_done, 1)
            x_low(0, 0)
            split_low(wu_lo, wu_raw, wu_hi, 0, wu_hi_done, wu_lo_done[0])
            add_bias(0, 0)
            find_top(0, 0)
            take_top(0, 0)
            select(0, 0)
            sum_up(0, 0)
            add_eps(0, 0)
            invert(0, 0)
            split_low(wd_lo, wd_raw, wd_hi, 0, wd_hi_done, wd_lo_done)
            stat(0, 1)
            aggr(0, 1)
            over_phases(dve, phase)
            dve.wait_ge(out_stored, 16 * (B - 1))
            last_sum(2 * B, B - 1)

        @block.tensor
        def _(pe):
            def keep_busy(n, o, a, b):
                for _ in range(n):
                    nc.tensor.matmul(o, a, b, start=True, stop=True)

            def split_product(o, a, b, start, stop):
                nc.tensor.matmul(o, a[0], b[0], start=start, stop=False)
                nc.tensor.matmul(o, a[0], b[1], start=False, stop=False)
                return nc.tensor.matmul(o, a[1], b[0], start=False, stop=stop)

            def small(a, b):
                return sm_hi[:, a:b], sm_lo[:, a:b]

            def turn(dst, src):
                for n in range(NB):
                    last = nc.tensor.transpose(rows(dst, n), src(n), ident[:, :])
                return last

            def turn_x(q, n, k, c):
                pe.wait_ge(norm_done[k], c + 1)
                turn(side1, lambda m: normed[k][:, m, :]).then_inc(x_turned[q], 1)

            def affinities(q, n):
                pe.wait_ge(x_lo_done[q], n + 1)
                for m in range(NB):
                    last = split_product(side1[:, m * E:(m + 1) * E], (rows(x_hi[q], m), rows(x_lo[q], m)),
                                         small(CE, CE + E), True, True)
                last.then_inc(aff_done[q], 1)

            def turn_cw(q, n):
                pe.wait_ge(dup_done[q], n + 1)
                turn(side0, lambda m: w_dup[:, m, :, :].rearrange("p e r -> p (e r)")).then_inc(cw_turned[q], 1)

            def turn_y(p):
                pe.wait_ge(y_copied, p)
                turn(side0, lambda m: rows(y_sb, m)).then_inc(y_turned, 1)

            def attention(c):
                pe.wait_ge(u_lo_done, c + 1)
                for m in range(NB):
                    o, a = att[:, m, 0:AW], m * P
                    edge = m in (0, NB - 1)
                    split_product(o, (u_hi[:, a:a + P], u_lo[:, a:a + P]), small(A1, A1 + AW), True, False)
                    last = split_product(o, (u_hi[:, a + 1:a + 1 + P], u_lo[:, a + 1:a + 1 + P]),
                                         small(A2, A2 + AW), False, not edge)
                    if m == 0:
                        last = split_product(o, (e0_hi[:, :], e0_lo[:, :]), small(I1, I1 + AW), False, True)
                    if m == NB - 1:
                        last = split_product(o, (e1_hi[:, :], e1_lo[:, :]), small(I2, I2 + AW), False, True)
                last.then_inc(att_done, 1)

            def up_product(ph, t):
                q, o = ph.q, up[t % RING]
                if t < NJ:
                    last = split_product(o[:, :], (wu_hi[:, t, :], wu_lo[:, t, :]), (x_hi[q][:, :], x_lo[q][:, :]), True, True)
                else:
                    for h in range(2):
                        s, a = SU + F * (1 - h), h * HT
                        last = split_product(o[:, 0:HT], small(s, s + P), (x_hi[q][:, a:a + HT], x_lo[q][:, a:a + HT]), h == 0, h == 1)
                last.then_inc(up_done, 1)

            def down_product(ph, t):
                made, t = low_count(ph, t), before(t)[1]
                pe.wait_ge(lo_done[t % 2], made)
                i, w = t % GRING, width(t)
                g = (g_hi[:, i, 0:w], g_lo[:, i, 0:w])
                if t < NJ:
                    last = split_product(y_ps[:, :], (wd_hi[:, t, :], wd_lo[:, t, :]), g, t == 0, False)
                else:
                    for h in range(2):
                        s, a = (SDL, SDH)[h], h * HT
                        last = split_product(y_ps[:, a:a + HT], small(s, s + D), g, False, h == 1)
                last.then_inc(down_done, 1)

            def free_bank(ph, t):
                back, tile = before(t)
                if tile % 2:
                    pe.wait_ge(gate_done, NJ * (ph.p - back) + tile + 1)
                else:
                    pe.wait_ge(lo_done[0], low_count(ph, t))

            def phase(ph):
                q = 1 - ph.q
                for t in range(SLOTS):
                    if ph.first and t % JP == LAG and t < NJ:
                        pe.wait_ge(wd_lo_done, t // JP + 1)
                    if before(t - LAG)[1] < NT and not (ph.first and t < LAG):
                        if t == LAG:
                            pe.wait_ge(y_copied, ph.p)
                        down_product(ph, t - LAG)
                    if ph.first and t < NJ and t % JP == 0:
                        pe.wait_ge(wu_lo_done[min(t, 1)], max(t // JP, 1))
                    if ph.first and t == NJ:
                        pe.wait_ge(sm_lo_done, 3)
                    if t == 0:
                        pe.wait_ge(x_lo_done[ph.q], ph.use + 1)
                    if t < NT and before(t - RING)[1] < NT and not (ph.first and t < RING):
                        free_bank(ph, t - RING)
                    if t < NT:
                        up_product(ph, t)
                    if ph.late and t == LATE:
                        if ph.first:
                            keep_busy(WARM_ROUTE, side0, wu_hi[:, 0, :], wu_hi[:, 0:NB, :])
                        turn_cw(ph.q, ph.use)
                    if ph.late and t == LATE + 1:
                        keep_busy(WARM_LATE, side1, wu_hi[:, 0, :], wu_hi[:, 0:NB, :])
                    if ph.at.get("v") == t:
                        pe.wait_ge(small_in[2], 80)
                        pe.wait_ge(cw_done[0], 1)
                        nc.tensor.matmul(side0[:, 256:258], wb_sb[:, :], sm_raw[:, I1 + D:I1 + AW], start=True, stop=True)
                        nc.tensor.matmul(side0[:, 258:260], wbf_sb[:, :], sm_raw[:, I2 + D:I2 + AW], start=True, stop=True).then_inc(v_done, 1)
                    if ph.at.get("x_t") == t:
                        turn_x(q, *ph.prep)
                    if ph.at.get("aff") == t:
                        affinities(q, ph.prep[0])
                    if ph.at.get("y_t") == t:
                        if ph.steady_a:
                            pe.wait_ge(t1_done, ph.norm2 + 1)
                        else:
                            pe.wait_ge(cw_done[ph.q], ph.use + 1)
                        turn_y(ph.p)
                    if ph.at.get("cw_t") == t:
                        if ph.steady_a:
                            pe.wait_ge(out_done, ph.post + 1)
                        if ph.first:
                            pe.wait_ge(v_copied, 2)
                        turn_cw(q, ph.prep[0])
                    if ph.at.get("u_t") == t:
                        if ph.steady_b:
                            pe.wait_ge(bias_done[q], ph.prep[0] + 1)
                        pe.wait_ge(norm_done[1], ph.mid + 1)
                        turn(side1, lambda m: normed[1][:, m, :]).then_inc(u_turned, 1)
                    if ph.at.get("attn") == t:
                        if ph.steady_b:
                            pe.wait_ge(cw_done[q], ph.prep[0] + 1)
                        attention(ph.mid)

            pe.wait_ge(consts_set, 1)
            keep_busy(WARM_START, side0, e0_hi[:, :], g_hi[:, 0, :])
            pe.wait_ge(small_in[0], 48)
            turn_x(0, 0, 0, 0)
            keep_busy(WARM_ROWS, side0, e0_hi[:, :], g_hi[:, 0, :])
            pe.wait_ge(sm_lo_done, 1)
            affinities(0, 0)
            over_phases(pe, phase)
            for t in range(SLOTS - LAG, NT):
                down_product(Phase(2 * B - 1, 1, {}), t)
            pe.wait_ge(out_done, B - 1)
            turn_y(2 * B)


def kernel(L0_attn_u, L0_attn_WA, L0_attn_WB, L0_attn_WAf, L0_attn_WBf, L0_attn_w1, L0_attn_w2, L0_attn_b, L0_attn_Wc,
           L0_ffn_centroids, L0_ffn_expert_biases, L0_ffn_Ws_up, L0_ffn_Ws_down, L0_ffn_W_up, L0_ffn_W_down):
    import numpy as np
    import concourse.bacc as bacc
    from concourse.bass_utils import run_bass_kernel_spmd

    def lay(a):
        return np.ascontiguousarray(a)

    WB, WBf = np.asarray(L0_attn_WB), np.asarray(L0_attn_WBf)
    w_up = np.asarray(L0_ffn_W_up).reshape(E, D, NJ, R).transpose(1, 2, 0, 3).reshape(D, NJ, P)
    w_down = np.asarray(L0_ffn_W_down).reshape(E, NJ, R, D).transpose(0, 2, 1, 3).reshape(P, NJ, D)
    arrays = {
        "x": lay(L0_attn_u), "ident": np.eye(P, dtype=np.float32), "cent_t": lay(np.asarray(L0_ffn_centroids).T),
        "ebias": lay(L0_ffn_expert_biases), "ws_up": lay(L0_ffn_Ws_up), "ws_down": lay(L0_ffn_Ws_down),
        "w_up": lay(w_up), "w_down": lay(w_down), "wb": lay(WB), "wb_t": lay(WB.T), "wbf": lay(WBf), "wbf_t": lay(WBf.T),
        "w1": lay(np.asarray(L0_attn_w1).reshape(D, 1)), "w2": lay(np.asarray(L0_attn_w2).reshape(D, 1)),
        "b": lay(L0_attn_b),
    }
    nc = bacc.Bacc("TRN2", target_bir_lowering=False, num_devices=1)
    args = [nc.dram_tensor(f"in_{k}", a.shape, mybir.dt.from_np(a.dtype), kind="ExternalInput").ap() for k, a in arrays.items()]
    out = nc.dram_tensor("out_0", (B, T, D), mybir.dt.float32, kind="ExternalOutput").ap()
    build(nc, *args, out)
    r = run_bass_kernel_spmd(nc, [{f"in_{k}": a for k, a in arrays.items()}], core_ids=[0])
    return r.results[0]["out_0"]
```

```python
from contextlib import ExitStack

import concourse.bass as bass
from concourse import mybir

B, T, D = 8, 512, 128
E, F, TOPK = 64, 64, 8
P = 128
NB = T // P
R = P // E
NJ = F // R
NT = NJ + 1
RING = 5
SLOTS = -(-NT // RING) * RING
LAG = RING + 1
GRING = LAG + 1
ORING = 4
NLOW = (NT // 2 + 1, NT // 2)
AW = D + 2
AS = 256
NPIECE = 4
JP = NJ // NPIECE
NSPLIT = 8
JS = NJ // NSPLIT
LN_EPS = 1e-5
SUM_EPS = 1e-8
WARM_START, WARM_ROWS, WARM_ROUTE = 12, 4, 7
TAKEN = -3.0e38


class Phase:

    def __init__(self, p, q, at, prep=None, norm0=None, mid=None, norm2=None, keep=None, post=None, first=False, use=None):
        self.p, self.q, self.at, self.first, self.late = p, q, at, first, at.get("late")
        self.use = p // 2 if isinstance(p, int) else use
        self.steady_a, self.steady_b = prep is not None and post is not None, prep is not None and mid is not None and norm2 is None
        self.prep, self.norm0, self.mid, self.norm2, self.keep, self.post = prep, norm0, mid, norm2, keep, post


NORM0 = ("stat0", "aggr0", "rstd0", "norm0")
AT_FIRST = {
    "x_t": 9, "x_hi": 10, "x_lo": 11, "aff": 14, "aff_sum": 14, "sig": 17, "bias": 16, "max": 18, "take": 19,
    "gate": 21, "sum": 22, "eps": 25, "inv": 27, "cw": 27, "cw_t": 33, "cw_copy": 33,
    "stat0": (1, 2), "aggr0": 3, "rstd0": 3, "norm0": (5, 6),
    "v": 11, "v_copy": 14, "wu_hi": (None, None, 2, 5, 8, 12, 15, 20),
    "wu_lo": (None, None, 3, 6, 9, 11, 17, 21), "wd_hi": (None, 4, 6, 12, 14, 19, 22, 26),
    "wd_lo": (None, 4, 8, 13, 16, 20, 24, 28),
    "late": 3,
}
AT_SECOND = {
    "x_t": 27, "x_hi": 28, "x_lo": 27, "aff": 33, "aff_sum": 31, "sig": 32, "bias": 31, "max": 31, "take": 32,
    "gate": 33, "sum": 33, "eps": 33, "inv": 33, "cw": 33,
    "y_t": 5, "x1": 6, "stat1": (7, 7), "aggr1": 8, "rstd1": 8, "norm1": (9, 10), "xu": 11, "u_t": 14,
    "u_copy": 12, "attn": 17, "tanh": 18, "gamma": 16, "t1": 18, "x2": (19, 19),
    "stat0": (0, 0), "aggr0": 3, "rstd0": 3, "norm0": (4, 5),
    "stat2": (20, 21), "aggr2": 21, "rstd2": 22, "norm2": (23, 23),
    "y": 3, "keep": 26,
}
AT_THIRD = {
    "x_t": 4, "x_hi": 6, "x_lo": 6, "aff": 10, "aff_sum": 10, "sig": 10, "bias": 10, "max": 14, "take": 15,
    "gate": 17, "sum": 19, "eps": 20, "inv": 21, "cw": 22, "cw_t": 26, "cw_copy": 26,
    "y_t": 6, "x1": 8, "stat1": (10, 12), "aggr1": 13, "rstd1": 14, "norm1": (16, 18), "xu": 19, "u_t": 22,
    "u_copy": 23, "attn": 29, "tanh": 29, "gamma": 30, "t1": 30, "x2": (32, 33),
    "stat2": (34, 34),
    "late": 3,
}
AT_STEADY_A = {
    "x_t": 7, "x_hi": 8, "x_lo": 10, "aff": 13, "aff_sum": 14, "sig": 15, "bias": 16, "max": 18, "take": 20,
    "gate": 22, "sum": 24, "eps": 26, "inv": 27, "cw": 28, "cw_t": 31, "cw_copy": 32,
    "y_t": 6,
    "stat0": (12, 14), "aggr0": 16, "rstd0": 17, "norm0": (28, 30),
    "aggr2": 0, "rstd2": 1, "norm2": (2, 4),
    "y": 2, "out": 8, "keep": 11,
}
AT_STEADY_B = {
    "x_t": 1, "x_hi": 2, "x_lo": 4, "aff": 8, "aff_sum": 8, "sig": 9, "bias": 10, "max": 14, "take": 15,
    "gate": 17, "sum": 19, "eps": 20, "inv": 21, "cw": 22, "cw_t": 26, "cw_copy": 26,
    "y_t": 6, "x1": 8, "stat1": (10, 12), "aggr1": 13, "rstd1": 14, "norm1": (16, 18), "xu": 19, "u_t": 22,
    "u_copy": 23, "attn": 28, "tanh": 29, "gamma": 30, "t1": 30, "x2": (32, 33),
    "stat2": (34, 34),
    "y": 2,
}
AT_MID_PREP = {
    "x_t": 27, "x_hi": 27, "x_lo": 27, "aff": 31, "aff_sum": 31, "sig": 32, "bias": 31, "max": 31, "take": 32,
    "gate": 32, "sum": 33, "eps": 33, "inv": 33, "cw": 33,
    "y_t": 5, "x1": 6, "stat1": (7, 7), "aggr1": 8, "rstd1": 8, "norm1": (9, 10), "xu": 10, "u_t": 14,
    "u_copy": 14, "attn": 17, "tanh": 18, "gamma": 16, "t1": 18, "x2": (19, 19),
    "stat2": (20, 21), "aggr2": 21, "rstd2": 22, "norm2": (23, 23),
    "y": 2,
}
AT_LAST = {
    "y_t": 4,
    "out": 4, "keep": 11, "late": 2,
}


def over_phases(eng, phase):
    phase(Phase(0, 0, AT_FIRST, prep=(0, 0, 1), norm0=1, first=True))
    phase(Phase(1, 1, AT_SECOND, mid=0, norm2=0, prep=(1, 2, 0), keep=0, norm0=2))
    phase(Phase(2, 0, AT_THIRD, prep=(1, 0, 2), mid=1))
    with eng.Fori(2, B - 1) as c:
        phase(Phase(2 * c - 1, 1, AT_STEADY_A, norm2=c - 1, post=c - 2, prep=(c, 2, c - 1), keep=c - 1, norm0=c + 1, use=c - 1))
        phase(Phase(2 * c, 0, AT_STEADY_B, prep=(c, 0, c + 1), mid=c, use=c))
    c = B - 1
    at = {k: v for k, v in AT_STEADY_A.items() if k not in NORM0}
    phase(Phase(2 * c - 1, 1, at, norm2=c - 1, post=c - 2, prep=(c, 2, c - 1), keep=c - 1))
    phase(Phase(2 * c, 0, AT_MID_PREP, mid=c, norm2=c, prep=(c, 2, c)))
    phase(Phase(2 * c + 1, 1, AT_LAST, post=c - 1, keep=c))


def build(nc, x, ident_in, cent_t, ebias, ws_up, ws_down, w_up, w_down, wb, wb_t, wbf, wbf_t, w1, w2, b_in, out):
    fp32, fp32r = mybir.dt.float32, mybir.dt.float32r
    ALU, ACT, AX = mybir.AluOpType, mybir.ActivationFunctionType, mybir.AxisListType
    ctx = ExitStack()
    with ctx:
        def sb(name, shape, dt=fp32):
            return ctx.enter_context(nc.sbuf_tensor(name, shape, dt))

        def sem(name):
            return ctx.enter_context(nc.semaphore(name))

        wu_raw, wd_raw = sb("wu_raw", [P, NJ, P]), sb("wd_raw", [P, NJ, P])
        wu_hi, wu_lo = sb("wu_hi", [P, NJ, P], fp32r), sb("wu_lo", [P, NJ, P], fp32r)
        wd_hi, wd_lo = sb("wd_hi", [P, NJ, P], fp32r), sb("wd_lo", [P, NJ, P], fp32r)
        SU, SD = 0, P
        A1, A2 = SD + D, SD + D + AW
        I1, I2 = A2 + AW, A2 + 2 * AW
        SW = I2 + AW
        sm_raw = sb("sm_raw", [P, SW])
        sm_hi, sm_lo = sb("sm_hi", [P, A1], fp32r), sb("sm_lo", [P, A1], fp32r)
        ce_raw = sb("ce_raw", [P, E])
        ce_both = sb("ce_both", [P, 2 * E], fp32r)
        wb_sb, wbf_sb = sb("wb_sb", [P, P]), sb("wbf_sb", [P, P])
        ident = sb("ident", [P, P])
        bias_b = sb("bias_b", [P, E])
        b_col, b_half = sb("b_col", [P, 1]), sb("b_half", [P, 1])
        neg_half = sb("neg_half", [P, NB])

        x_hi = [sb(f"x_hi{q}", [P, T], fp32r) for q in range(2)]
        x_lo = [sb(f"x_lo{q}", [P, T], fp32r) for q in range(2)]
        cw = [sb(f"cw{q}", [P, T]) for q in range(2)]
        gated = sb("gated", [P, ORING, T])
        g_hi, g_lo = sb("g_hi", [P, GRING, T], fp32r), sb("g_lo", [P, GRING, T], fp32r)

        x_in, x_res = sb("x_in", [P, NB, D]), sb("x_res", [P, NB, D])
        x1, x2, x2_kept = sb("x1", [P, NB, D]), sb("x2", [P, NB, D]), sb("x2_kept", [P, NB, D])
        out_sb = sb("out_sb", [P, NB, D])
        normed = [sb(f"normed{k}", [P, NB, D]) for k in range(3)]
        xu, t1 = sb("xu", [P, NB, D]), sb("t1", [P, NB, D])
        y_sb = sb("y_sb", [P, T])
        stats = [sb(f"stats{k}", [P, NB, 6]) for k in range(3)]
        mv = [sb(f"mv{k}", [P, NB, 2]) for k in range(3)]
        var_eps = [sb(f"var_eps{k}", [P, NB]) for k in range(3)]
        rstd = [sb(f"rstd{k}", [P, NB]) for k in range(3)]
        th, gamma = sb("th", [P, NB]), sb("gamma", [P, NB])
        u_mid = sb("u_mid", [P, T + 2])
        e0, e1 = sb("e0", [P, P]), sb("e1", [P, P])
        zeros_r = sb("zeros_r", [P, P], fp32r)
        aff = sb("aff", [P, NB, E])
        sig, biased, taken = sb("sig", [P, NB, E]), sb("biased", [P, NB, E]), sb("taken", [P, NB, E])
        top = sb("top", [P, NB, TOPK])
        w_sel, w_dup = sb("w_sel", [P, NB, E]), sb("w_dup", [P, NB, E, R])
        w_sum, w_eps, w_inv = sb("w_sum", [P, NB]), sb("w_eps", [P, NB]), sb("w_inv", [P, NB])

        up = [ctx.enter_context(nc.psum_tensor(f"up{i}", [P, T], fp32)) for i in range(RING)]
        y_ps = ctx.enter_context(nc.psum_tensor("y_ps", [P, T], fp32))
        side = ctx.enter_context(nc.psum_tensor("side", [P, 2 * T], fp32))
        side0, side1 = side[:, 0:T], side[:, T:2 * T]
        att = side[:, :].rearrange("p (n c) -> p n c", c=AS)
        side_rows = [s.rearrange("p (n d) -> p n d", n=NB) for s in (side0, side1)]

        small_in = [sem(f"small_in{i}") for i in range(4)]
        wu_in, wd_in = [sem(f"wu_in{i}") for i in range(NPIECE)], [sem(f"wd_in{i}") for i in range(NPIECE)]
        consts_set, v_done, sm_hi_done, sm_lo_done = (sem(s) for s in ("consts_set", "v_done", "sm_hi_done", "sm_lo_done"))
        ce_hi_done, ce_lo_done = sem("ce_hi_done"), sem("ce_lo_done")
        v_copied, half_b_done = sem("v_copied"), sem("half_b_done")
        wu_hi_done, wd_hi_done, wd_lo_done = sem("wu_hi_done"), sem("wd_hi_done"), sem("wd_lo_done")
        wu_lo_done = [sem("wu_lo_done_vector"), sem("wu_lo_done_pool")]
        up_done, silu_done, gate_done, hi_done = (sem(s) for s in ("up_done", "silu_done", "gate_done", "hi_done"))
        lo_done = [sem("lo_done_vector"), sem("lo_done_pool")]
        down_done, y_copied, y_turned = sem("down_done"), sem("y_copied"), sem("y_turned")
        x_in_done, x_res_done, out_stored = sem("x_in_done"), sem("x_res_done"), sem("out_stored")
        stat_done, mv_done = [sem(f"stat_done{k}") for k in range(3)], [sem(f"mv_done{k}") for k in range(3)]
        eps_done, rstd_done = [sem(f"eps_done{k}") for k in range(3)], [sem(f"rstd_done{k}") for k in range(3)]
        norm_done = [sem(f"norm_done{k}") for k in range(3)]

        def pair(name):
            return [sem(f"{name}{q}") for q in range(2)]

        x_turned, x_hi_done, x_lo_done, aff_done = pair("x_turned"), pair("x_hi_done"), pair("x_lo_done"), pair("aff_done")
        aff_summed = pair("aff_summed")
        sig_done, bias_done, top_done, taken_done = pair("sig_done"), pair("bias_done"), pair("top_done"), pair("taken_done")
        sel_done, sum_done, sum_eps_done, inv_done = pair("sel_done"), pair("sum_done"), pair("sum_eps_done"), pair("inv_done")
        first_dup_done = sem("first_dup_done")
        dup_done, cw_turned, cw_done = pair("dup_done"), pair("cw_turned"), pair("cw_done")
        x1_done, xu_done, u_turned, u_copied = (sem(s) for s in ("x1_done", "xu_done", "u_turned", "u_copied"))
        att_done, tanh_done, gamma_done, t1_done = (sem(s) for s in ("att_done", "tanh_done", "gamma_done", "t1_done"))
        x2_done, kept_done, out_done = sem("x2_done"), sem("kept_done"), sem("out_done")

        held, power_set = sem("held"), sem("power_set")

        norm_from = [x_in, x1, x2]
        norm_from_done = [None, x1_done, x2_done]

        def before(t):
            return (0, t) if t >= 0 else (1, t + SLOTS)

        def low_count(ph, t):
            back, t = before(t)
            return NLOW[t % 2] * (ph.p - back) + t // 2 + 1

        def halves(ph, name, t):
            at = ph.at.get(name, ())
            blocks = [n for h, a in enumerate(at) if a == t for n in range(h * NB // 2, (h + 1) * NB // 2)]
            return blocks, bool(blocks) and blocks[-1] == NB - 1

        def half(h, n):
            return slice(h * n // 2, (h + 1) * n // 2)

        def hold(eng, s, value):
            eng.wait_ge(s, value)
            if not isinstance(value, int):
                eng.sem_inc(held, 1)

        def rows(ap, n):
            return ap[:, n * P:(n + 1) * P]

        spread_operands = (w_dup[:, :, :, :], w_sel[:, :, :].unsqueeze(3).to_broadcast([P, NB, E, R]),
                           w_inv[:, :].unsqueeze(2).unsqueeze(3).to_broadcast([P, NB, E, R]))

        block = ctx.enter_context(nc.Block())

        @block.sync
        def _(sp):
            def rows_of(dram, c):
                return dram[bass.ds(c, 1), :, :].rearrange("o (n p) d -> p (o n) d", p=P)

            def load_x(c, wait=True):
                if wait:
                    sp.wait_ge(norm_done[0], c)
                sp.dma_start(x_in[:, :, :], rows_of(x, c)).then_inc(x_in_done, 16)

            def load_res(c, wait=True):
                if wait:
                    sp.wait_ge(x1_done, c)
                sp.dma_start(x_res[:, :, :], rows_of(x, c)).then_inc(x_res_done, 16)

            def store(c):
                sp.wait_ge(out_done, c + 1)
                sp.dma_start(rows_of(out, c), out_sb[:, :, :]).then_inc(out_stored, 16)

            def load_pieces(i):
                js = slice(i * JP, (i + 1) * JP)
                sp.dma_start(wu_raw[:, js, :], w_up[:, js, :]).then_inc(wu_in[i], 16)
                sp.dma_start(wd_raw[:, js, :], w_down[:, js, :]).then_inc(wd_in[i], 16)

            load_x(0, wait=False)
            sp.dma_start(ce_raw[:, :], cent_t).then_inc(small_in[0], 16)
            sp.dma_start(ident[:, :], ident_in).then_inc(small_in[0], 16)
            sp.dma_start(bias_b[:, :], ebias.partition_broadcast(P)).then_inc(small_in[0], 16)
            for h in range(2):
                sp.dma_start(sm_raw[:, SU + h * F:SU + (h + 1) * F], ws_up).then_inc(small_in[1], 16)
                sp.dma_start(sm_raw[h * F:(h + 1) * F, SD:SD + D], ws_down).then_inc(small_in[1], 16)
            load_pieces(0)
            load_pieces(1)
            load_x(1)
            sp.dma_start(wb_sb[:, :], wb).then_inc(small_in[2], 16)
            sp.dma_start(wbf_sb[:, :], wbf).then_inc(small_in[2], 16)
            sp.dma_start(b_col[:, :], b_in.partition_broadcast(P)).then_inc(small_in[2], 16)
            sp.wait_ge(consts_set, 1)
            sp.dma_start(sm_raw[:, I1 + D:I1 + D + 1], w1).then_inc(small_in[2], 16)
            sp.dma_start(sm_raw[:, I2 + D:I2 + D + 1], w2).then_inc(small_in[2], 16)
            load_pieces(2)
            sp.dma_start(sm_raw[:, A1:A1 + D], wb_t).then_inc(small_in[3], 16)
            sp.dma_start(sm_raw[:, A2:A2 + D], wbf_t).then_inc(small_in[3], 16)
            sp.dma_start(sm_raw[:, I1:I1 + D], ident_in).then_inc(small_in[3], 16)
            sp.dma_start(sm_raw[:, I2:I2 + D], ident_in).then_inc(small_in[3], 16)
            load_pieces(3)
            load_res(0, wait=False)
            load_x(2)
            load_res(1)
            with sp.Fori(2, B - 1) as c:
                load_x(c + 1)
                store(c - 2)
                sp.wait_ge(out_stored, 16 * (c - 1))
                load_res(c)
            store(B - 3)
            sp.wait_ge(out_stored, 16 * (B - 2))
            load_res(B - 1)
            store(B - 2)
            for h in range(2):
                sp.wait_ge(out_done, B + h)
                sp.dma_start(rows_of(out, B - 1)[:, half(h, NB), :], out_sb[:, half(h, NB), :]).then_inc(out_stored, 16)
            sp.wait_ge(out_stored, 16 * (B + 1))

        @block.gpsimd
        def _(pool):
            def rstd_of(k, c):
                hold(pool, mv_done[k], c + 1)
                nc.gpsimd.tensor_scalar_add(var_eps[k][:, :], mv[k][:, :, 1], LN_EPS).then_inc(eps_done[k], 1)
                pool.wait_ge(eps_done[k], c + 1)
                nc.gpsimd.tensor_tensor(rstd[k][:, :], var_eps[k][:, :], neg_half[:, :], ALU.pow).then_inc(rstd_done[k], 1)

            def spread(q, n):
                pool.wait_ge(inv_done[q], n + 1)
                nc.gpsimd.tensor_tensor(*spread_operands, ALU.mult).then_inc(dup_done[q], 1)

            def low_part(ph, t):
                i = t % GRING
                pool.wait_ge(hi_done, NT * ph.p + t + 1)
                nc.gpsimd.tensor_tensor(g_lo[:, i, :], gated[:, t // 2 % ORING, :], g_hi[:, i, :].bitcast(fp32),
                                        ALU.subtract).then_inc(lo_done[1], 1)

            def split_up(i):
                js = slice(i * JS, (i + 1) * JS)
                pool.wait_ge(wu_hi_done, i + 1)
                nc.gpsimd.tensor_tensor(wu_lo[:, js, :], wu_raw[:, js, :], wu_hi[:, js, :].bitcast(fp32),
                                        ALU.subtract).then_inc(wu_lo_done[1], 1)

            def phase(ph):
                for t in range(SLOTS):
                    if (t - 1) % 2 and 0 < t <= NT:
                        low_part(ph, t - 1)
                    if t in ph.at.get("wu_lo", ()):
                        split_up(ph.at["wu_lo"].index(t))
                    for k, c in ((0, ph.norm0), (1, ph.mid), (2, ph.norm2)):
                        if ph.at.get(f"rstd{k}") == t:
                            rstd_of(k, c)
                    if ph.at.get("xu") == t:
                        pool.wait_ge(norm_done[1], ph.mid + 1)
                        nc.gpsimd.tensor_tensor(xu[:, :, :], x1[:, :, :], normed[1][:, :, :], ALU.add).then_inc(xu_done, 1)
                    if ph.at.get("gamma") == t:
                        hold(pool, tanh_done, ph.mid + 1)
                        nc.gpsimd.tensor_scalar(gamma[:, :], th[:, :], 0.5, 0.5, ALU.mult, ALU.add).then_inc(gamma_done, 1)
                    if ph.at.get("keep") == t:
                        if ph.post is not None:
                            pool.wait_ge(out_done, ph.post + 1)
                        hold(pool, x2_done, ph.keep + 1)
                        nc.gpsimd.tensor_copy(x2_kept[:, :, :], x2[:, :, :]).then_inc(kept_done, 1)
                    if ph.at.get("cw") == t:
                        spread(1 - ph.q, ph.prep[0])

            nc.gpsimd.memset(neg_half[:, :], -0.5).then_inc(power_set, 1)
            pool.wait_ge(power_set, 1)
            rstd_of(0, 0)
            split_up(1)
            over_phases(pool, phase)

        @block.scalar
        def _(act):
            def x_high(q, n):
                act.wait_ge(x_turned[q], n + 1)
                nc.scalar.copy(x_hi[q][:, :], side1).then_inc(x_hi_done[q], 1)

            def sigmoid(q, n):
                act.wait_ge(aff_summed[q], n + 1)
                nc.scalar.activation(sig[:, :, :], aff[:, :, :], ACT.Sigmoid).then_inc(sig_done[q], 1)

            def cw_copy(q, n):
                act.wait_ge(cw_turned[q], n + 1)
                nc.scalar.copy(cw[q][:, :], side0).then_inc(cw_done[q], 1)

            def silu(ph, t):
                i = t % RING
                act.wait_ge(up_done, NT * ph.p + t + 1)
                nc.scalar.activation(up[i][:, :], up[i][:, :], ACT.Silu).then_inc(silu_done, 1)

            def high_part(ph, t):
                if t > 0:
                    act.wait_ge(gate_done, NJ * ph.p + t)
                else:
                    act.wait_ge(silu_done, NT * ph.p + t + 1)
                src = gated[:, t // 2 % ORING, :] if t % 2 else up[t % RING][:, :]
                nc.scalar.copy(g_hi[:, t % GRING, :], src).then_inc(hi_done, 1)

            def y_copy(p):
                act.wait_ge(down_done, NT * p)
                act.wait_ge(y_turned, p - 1)
                nc.scalar.copy(y_sb[:, :], y_ps[:, :]).then_inc(y_copied, 1)

            def u_copy(c):
                act.wait_ge(u_turned, c + 1)
                nc.scalar.copy(u_mid[:, 1:T], side1[:, 1:T])
                nc.scalar.copy(e0[:, 0:1], side1[:, 0:1])
                nc.scalar.copy(e1[:, P - 1:P], side1[:, T - 1:T]).then_inc(u_copied, 1)

            def phase(ph):
                if ph.late is not None:
                    for t in range(ph.late + 1):
                        silu(ph, t)
                        if t == 1:
                            high_part(ph, 0)
                    cw_copy(ph.q, ph.use)
                    if not ph.first:
                        y_copy(ph.p)
                for t in range(SLOTS):
                    if t < NT and (ph.late is None or t > ph.late):
                        silu(ph, t)
                    if t <= NT and t > (ph.late is not None):
                        high_part(ph, t - 1)
                    if t in ph.at.get("wu_hi", ()):
                        split_up(ph.at["wu_hi"].index(t))
                    if t in ph.at.get("wd_hi", ()):
                        split_down(ph.at["wd_hi"].index(t))
                    if ph.at.get("y") == t:
                        y_copy(ph.p)
                    if ph.at.get("x_hi") == t:
                        x_high(1 - ph.q, ph.prep[0])
                    if ph.at.get("sig") == t:
                        sigmoid(1 - ph.q, ph.prep[0])
                    if ph.at.get("cw_copy") == t:
                        cw_copy(1 - ph.q, ph.prep[0])
                    if ph.at.get("u_copy") == t:
                        u_copy(ph.mid)
                    if ph.at.get("tanh") == t:
                        act.wait_ge(att_done, ph.mid + 1)
                        nc.scalar.activation(th[:, :].unsqueeze(2), att[:, :, D:D + 1], ACT.Tanh, bias=b_half[:, :],
                                             scale=0.5).then_inc(tanh_done, 1)

            def split_up(i):
                js = slice(i * JS, (i + 1) * JS)
                act.wait_ge(wu_in[i * NPIECE // NSPLIT], 16)
                nc.scalar.copy(wu_hi[:, js, :], wu_raw[:, js, :]).then_inc(wu_hi_done, 1)

            def split_down(i):
                js = slice(i * JS, (i + 1) * JS)
                act.wait_ge(wd_in[i * NPIECE // NSPLIT], 16)
                nc.scalar.copy(wd_hi[:, js, :], wd_raw[:, js, :]).then_inc(wd_hi_done, 1)

            act.wait_ge(power_set, 1)
            nc.scalar.activation(th[:, :], neg_half[:, :], ACT.Sigmoid)
            act.wait_ge(small_in[0], 48)
            nc.scalar.copy(ce_both[:, 0:E], ce_raw[:, :]).then_inc(ce_hi_done, 1)
            act.wait_ge(small_in[1], 64)
            nc.scalar.copy(sm_hi[:, :], sm_raw[:, 0:A1]).then_inc(sm_hi_done, 1)
            x_high(0, 0)
            split_up(0)
            split_up(1)
            split_down(0)
            sigmoid(0, 0)
            over_phases(act, phase)
            for h in range(2):
                act.wait_ge(down_done, 2 * B * NT)
                act.wait_ge(y_turned, 2 * B - 1)
                nc.scalar.copy(y_sb[:, half(h, T)], y_ps[:, half(h, T)]).then_inc(y_copied, 1)

        @block.vector
        def _(dve):
            def stat(k, c, blocks=range(NB), last=True):
                if k == 0:
                    dve.wait_ge(x_in_done, 16 * (c + 1))
                else:
                    dve.wait_ge(norm_from_done[k], c + 1)
                for n in blocks:
                    made = nc.vector.bn_stats(stats[k][:, n, :], norm_from[k][:, n, :])
                if last:
                    made.then_inc(stat_done[k], 1)

            def aggr(k, c):
                hold(dve, stat_done[k], c + 1)
                for n in range(NB):
                    last = nc.vector.bn_aggr(mv[k][:, n, :], stats[k][:, n, :])
                last.then_inc(mv_done[k], 1)

            def norm(k, c, blocks=range(NB), last=True):
                dve.wait_ge(rstd_done[k], c + 1)
                for n in blocks:
                    made = nc.vector.tensor_scalar(normed[k][:, n, :], norm_from[k][:, n, :], mv[k][:, n, 0:1],
                                                   rstd[k][:, n:n + 1], ALU.subtract, ALU.mult)
                if last:
                    made.then_inc(norm_done[k], 1)

            def x_low(q, n):
                dve.wait_ge(x_hi_done[q], n + 1)
                nc.vector.tensor_tensor(x_lo[q][:, :], side1, x_hi[q][:, :].bitcast(fp32), ALU.subtract).then_inc(x_lo_done[q], 1)

            def sum_aff(q, n):
                dve.wait_ge(aff_done[q], n + 1)
                nc.vector.reduce_sum(aff[:, :, :], side1.rearrange("p (n h e) -> p n e h", n=NB, h=2), axis=AX.X).then_inc(aff_summed[q], 1)

            def add_bias(q, n):
                dve.wait_ge(aff_summed[q], n + 1)
                nc.vector.tensor_tensor(biased[:, :, :], aff[:, :, :],
                                        bias_b[:, :].unsqueeze(1).to_broadcast([P, NB, E]), ALU.add).then_inc(bias_done[q], 1)

            def find_top(q, n):
                hold(dve, bias_done[q], n + 1)
                for m in range(NB):
                    last = nc.vector.max(top[:, m, :], biased[:, m, :])
                last.then_inc(top_done[q], 1)

            def take_top(q, n):
                hold(dve, top_done[q], n + 1)
                for m in range(NB):
                    last = nc.vector.match_replace(taken[:, m, :], top[:, m, :], biased[:, m, :], TAKEN)
                last.then_inc(taken_done[q], 1)

            def select(q, n):
                dve.wait_ge(sig_done[q], n + 1)
                dve.wait_ge(taken_done[q], n + 1)
                nc.vector.scalar_tensor_tensor(w_sel[:, :, :], taken[:, :, :], TAKEN, sig[:, :, :],
                                               ALU.is_equal, ALU.mult).then_inc(sel_done[q], 1)

            def sum_up(q, n):
                dve.wait_ge(sel_done[q], n + 1)
                nc.vector.reduce_sum(w_sum[:, :], w_sel[:, :, :], axis=AX.X).then_inc(sum_done[q], 1)

            def add_eps(q, n):
                dve.wait_ge(sum_done[q], n + 1)
                nc.vector.tensor_scalar_add(w_eps[:, :], w_sum[:, :], SUM_EPS).then_inc(sum_eps_done[q], 1)

            def invert(q, n):
                dve.wait_ge(sum_eps_done[q], n + 1)
                nc.vector.reciprocal(w_inv[:, :], w_eps[:, :]).then_inc(inv_done[q], 1)

            def gate(ph, t):
                i = t % RING
                dve.wait_ge(silu_done, NT * ph.p + t + 1)
                nc.vector.tensor_tensor(gated[:, t // 2 % ORING, :] if t % 2 else up[i][:, :], up[i][:, :], cw[ph.q][:, :],
                                        ALU.mult).then_inc(gate_done, 1)

            def low_part(ph, t):
                i = t % GRING
                ps, lo = (slice(0, P), g_lo) if t > 0 else (slice(F, P), g_hi)
                dve.wait_ge(hi_done, NT * ph.p + t + 1)
                nc.vector.tensor_tensor(lo[ps, i, :], up[t % RING][ps, :], g_hi[ps, i, :].bitcast(fp32),
                                        ALU.subtract).then_inc(lo_done[0], 1)

            def split_low(lo, raw, hi, i, made, done):
                js = slice(i * JS, (i + 1) * JS)
                dve.wait_ge(made, i + 1)
                nc.vector.tensor_tensor(lo[:, js, :], raw[:, js, :], hi[:, js, :].bitcast(fp32),
                                        ALU.subtract).then_inc(done, 1)

            def last_sum(p, c):
                dve.wait_ge(y_turned, p)
                dve.wait_ge(kept_done, c + 1)
                nc.vector.scalar_tensor_tensor(out_sb[:, :, :], side_rows[0], 0.5, x2_kept[:, :, :],
                                               ALU.mult, ALU.add).then_inc(out_done, 1)

            def phase(ph):
                q = 1 - ph.q
                n = ph.prep[0] if ph.prep else None
                for t in range(SLOTS):
                    if t == 1:
                        low_part(ph, 0)
                        dve.wait_ge(cw_done[ph.q], ph.use + 1)
                    if 0 < t < NT:
                        gate(ph, t)
                    if t % 2 and 1 < t <= NT:
                        low_part(ph, t - 1)
                    if t in ph.at.get("wd_lo", ()):
                        split_low(wd_lo, wd_raw, wd_hi, ph.at["wd_lo"].index(t), wd_hi_done, wd_lo_done)
                    if ph.at.get("v_copy") == t:
                        dve.wait_ge(small_in[2], 80)
                        nc.vector.tensor_scalar_mul(b_half[:, :], b_col[:, :], 0.5).then_inc(half_b_done, 1)
                        dve.wait_ge(v_done, 1)
                        nc.vector.tensor_copy(sm_raw[:, A1 + D:A1 + AW], side0[:, 256:258]).then_inc(v_copied, 1)
                        nc.vector.tensor_copy(sm_raw[:, A2 + D:A2 + AW], side0[:, 258:260]).then_inc(v_copied, 1)
                    for k, c in ((0, ph.norm0), (1, ph.mid), (2, ph.norm2 if ph.norm2 is not None else ph.mid)):
                        blocks, last = halves(ph, f"stat{k}", t)
                        if blocks:
                            stat(k, c, blocks, last)
                        if ph.at.get(f"aggr{k}") == t:
                            aggr(k, c)
                        blocks, last = halves(ph, f"norm{k}", t)
                        if blocks:
                            norm(k, c, blocks, last)
                    for name, step in (("x_lo", x_low), ("aff_sum", sum_aff), ("bias", add_bias), ("max", find_top), ("take", take_top),
                                       ("gate", select), ("sum", sum_up), ("eps", add_eps), ("inv", invert)):
                        if ph.at.get(name) == t:
                            step(q, n)
                    if ph.at.get("x1") == t:
                        dve.wait_ge(y_turned, ph.p)
                        dve.wait_ge(x_res_done, 16 * (ph.mid + 1))
                        nc.vector.scalar_tensor_tensor(x1[:, :, :], side_rows[0], 0.5, x_res[:, :, :],
                                                       ALU.mult, ALU.add).then_inc(x1_done, 1)
                    if ph.at.get("t1") == t:
                        dve.wait_ge(tanh_done, ph.mid + 1)
                        nc.vector.tensor_tensor(t1[:, :, :], att[:, :, 0:D], normed[1][:, :, :],
                                                ALU.subtract).then_inc(t1_done, 1)
                    blocks, last = halves(ph, "x2", t)
                    if blocks:
                        dve.wait_ge(t1_done, ph.mid + 1)
                        dve.wait_ge(gamma_done, ph.mid + 1)
                        dve.wait_ge(xu_done, ph.mid + 1)
                        dve.wait_ge(kept_done, ph.mid)
                        for m in blocks:
                            made = nc.vector.scalar_tensor_tensor(x2[:, m, :], t1[:, m, :], gamma[:, m:m + 1], xu[:, m, :],
                                                                  ALU.mult, ALU.add)
                        if last:
                            made.then_inc(x2_done, 1)
                    if ph.at.get("out") == t:
                        last_sum(ph.p, ph.post)

            nc.vector.memset(sm_raw[:, I1 + D:I1 + AW], 0.0)
            nc.vector.memset(sm_raw[:, I2 + D:I2 + AW], 0.0)
            nc.vector.memset(u_mid[:, 0:1], 0.0)
            nc.vector.memset(u_mid[:, T:T + 2], 0.0)
            nc.vector.memset(g_hi[:, 0, :].bitcast(fp32), 0.0)
            nc.vector.memset(zeros_r[:, :].bitcast(fp32), 0.0)
            for edge in (e0, e1):
                last = nc.vector.memset(edge[:, :], 0.0)
            last.then_inc(consts_set, 1)
            stat(0, 0)
            aggr(0, 0)
            norm(0, 0)
            dve.wait_ge(ce_hi_done, 1)
            nc.vector.tensor_tensor(ce_both[:, E:2 * E], ce_raw[:, :], ce_both[:, 0:E].bitcast(fp32),
                                    ALU.subtract).then_inc(ce_lo_done, 1)
            x_low(0, 0)
            dve.wait_ge(sm_hi_done, 1)
            nc.vector.tensor_tensor(sm_lo[:, :], sm_raw[:, 0:A1], sm_hi[:, :].bitcast(fp32), ALU.subtract).then_inc(sm_lo_done, 1)
            split_low(wu_lo, wu_raw, wu_hi, 0, wu_hi_done, wu_lo_done[0])
            sum_aff(0, 0)
            add_bias(0, 0)
            find_top(0, 0)
            take_top(0, 0)
            select(0, 0)
            sum_up(0, 0)
            add_eps(0, 0)
            invert(0, 0)
            dve.wait_ge(inv_done[0], 1)
            nc.vector.tensor_tensor(*spread_operands, ALU.mult).then_inc(first_dup_done, 1)
            split_low(wd_lo, wd_raw, wd_hi, 0, wd_hi_done, wd_lo_done)
            over_phases(dve, phase)
            dve.wait_ge(out_stored, 16 * (B - 1))
            dve.wait_ge(kept_done, B)
            for h in range(2):
                dve.wait_ge(y_turned, 2 * B + h)
                nc.vector.scalar_tensor_tensor(out_sb[:, half(h, NB), :], side_rows[h][:, half(h, NB), :], 0.5,
                                               x2_kept[:, half(h, NB), :], ALU.mult, ALU.add).then_inc(out_done, 1)

        @block.tensor
        def _(pe):
            def keep_busy(n, o, a, b):
                for _ in range(n):
                    nc.tensor.matmul(o, a, b, start=True, stop=True)

            def split_product(o, a, b, start, stop):
                nc.tensor.matmul(o, a[0], b[0], start=start, stop=False)
                nc.tensor.matmul(o, a[0], b[1], start=False, stop=False)
                return nc.tensor.matmul(o, a[1], b[0], start=False, stop=stop)

            def small(a, b):
                return sm_hi[:, a:b], sm_lo[:, a:b]

            def turn(dst, src):
                for n in range(NB):
                    last = nc.tensor.transpose(rows(dst, n), src(n), ident[:, :])
                return last

            def turn_x(q, n, k, c):
                pe.wait_ge(norm_done[k], c + 1)
                turn(side1, lambda m: normed[k][:, m, :]).then_inc(x_turned[q], 1)

            def affinities(q, n):
                pe.wait_ge(x_lo_done[q], n + 1)
                for m in range(NB):
                    nc.tensor.matmul(rows(side1, m), rows(x_hi[q], m), ce_both[:, :], start=True, stop=False)
                    last = nc.tensor.matmul(side1[:, m * P:m * P + E], rows(x_lo[q], m), ce_both[:, 0:E], start=False, stop=True)
                last.then_inc(aff_done[q], 1)

            def turn_cw(q, n, first=False):
                if first:
                    pe.wait_ge(first_dup_done, 1)
                else:
                    pe.wait_ge(dup_done[q], n + 1 - (q == 0))
                turn(side0, lambda m: w_dup[:, m, :, :].rearrange("p e r -> p (e r)")).then_inc(cw_turned[q], 1)

            def turn_y(p):
                pe.wait_ge(y_copied, p)
                turn(side0, lambda m: rows(y_sb, m)).then_inc(y_turned, 1)

            def attention(c):
                pe.wait_ge(u_copied, c + 1)
                for m in range(NB):
                    o, a = att[:, m, 0:AW], m * P
                    edge = m in (0, NB - 1)
                    nc.tensor.matmul(o, u_mid[:, a:a + P], sm_raw[:, A1:A1 + AW], start=True, stop=False)
                    last = nc.tensor.matmul(o, u_mid[:, a + 1:a + 1 + P], sm_raw[:, A2:A2 + AW], start=False, stop=not edge)
                    if m == 0:
                        last = nc.tensor.matmul(o, e0[:, :], sm_raw[:, I1:I1 + AW], start=False, stop=True)
                    if m == NB - 1:
                        last = nc.tensor.matmul(o, e1[:, :], sm_raw[:, I2:I2 + AW], start=False, stop=True)
                last.then_inc(att_done, 1)

            def up_product(ph, t):
                q, o = ph.q, up[t % RING]
                w = (wu_hi[:, t - 1, :], wu_lo[:, t - 1, :]) if t > 0 else small(SU, SU + P)
                split_product(o[:, :], w, (x_hi[q][:, :], x_lo[q][:, :]), True, True).then_inc(up_done, 1)

            def down_product(ph, t):
                made, t = low_count(ph, t), before(t)[1]
                pe.wait_ge(lo_done[t % 2], made)
                i = t % GRING
                if t > 0:
                    last = split_product(y_ps[:, :], (wd_hi[:, t - 1, :], wd_lo[:, t - 1, :]), (g_hi[:, i, :], g_lo[:, i, :]),
                                         False, t == NT - 1)
                else:
                    nc.tensor.matmul(y_ps[:, :], sm_hi[:, SD:SD + D], g_hi[:, i, :], start=True, stop=False)
                    last = nc.tensor.matmul(y_ps[:, :], sm_lo[:, SD:SD + D], g_hi[:, i, :], start=False, stop=False)
                last.then_inc(down_done, 1)

            def free_bank(ph, t):
                back, tile = before(t)
                if tile % 2:
                    pe.wait_ge(gate_done, NJ * (ph.p - back) + tile)
                else:
                    pe.wait_ge(lo_done[0], low_count(ph, t))

            def phase(ph):
                q = 1 - ph.q
                for t in range(SLOTS):
                    if ph.first and t > LAG and (t - LAG - 1) % JS == 0 and t - LAG < NT:
                        pe.wait_ge(wd_lo_done, (t - LAG - 1) // JS + 1)
                    if before(t - LAG)[1] < NT and not (ph.first and t < LAG):
                        if t == LAG:
                            pe.wait_ge(y_copied, ph.p)
                        down_product(ph, t - LAG)
                    if ph.first and 0 < t < NT and (t - 1) % JS == 0:
                        i = (t - 1) // JS
                        pe.wait_ge(wu_lo_done[min(i, 1)], max(i, 1))
                    if ph.first and t == 0:
                        pe.wait_ge(sm_lo_done, 1)
                    if ph.first and t == NJ:
                        pe.wait_ge(small_in[3], 64)
                    if t == 0:
                        pe.wait_ge(x_lo_done[ph.q], ph.use + 1)
                    if t < NT and before(t - RING)[1] < NT and not (ph.first and t < RING):
                        free_bank(ph, t - RING)
                    if t < NT:
                        up_product(ph, t)
                    if ph.late == t:
                        if ph.first:
                            keep_busy(WARM_ROUTE, side0, wu_hi[:, 0, :], wu_hi[:, 0:NB, :])
                        turn_cw(ph.q, ph.use, ph.first)
                    if ph.at.get("v") == t:
                        pe.wait_ge(small_in[2], 80)
                        pe.wait_ge(cw_done[0], 1)
                        nc.tensor.matmul(side0[:, 256:258], wb_sb[:, :], sm_raw[:, I1 + D:I1 + AW], start=True, stop=True)
                        nc.tensor.matmul(side0[:, 258:260], wbf_sb[:, :], sm_raw[:, I2 + D:I2 + AW], start=True, stop=True).then_inc(v_done, 1)
                    if ph.at.get("x_t") == t:
                        turn_x(q, *ph.prep)
                    if ph.at.get("aff") == t:
                        affinities(q, ph.prep[0])
                    if ph.at.get("y_t") == t:
                        if ph.steady_a:
                            pe.wait_ge(t1_done, ph.norm2 + 1)
                        else:
                            pe.wait_ge(cw_done[ph.q], ph.use + 1)
                        turn_y(ph.p)
                    if ph.at.get("cw_t") == t:
                        if ph.steady_a:
                            pe.wait_ge(out_done, ph.post + 1)
                        if ph.first:
                            pe.wait_ge(v_copied, 2)
                        turn_cw(q, ph.prep[0])
                    if ph.at.get("u_t") == t:
                        if ph.steady_b:
                            pe.wait_ge(aff_summed[q], ph.prep[0] + 1)
                        pe.wait_ge(norm_done[1], ph.mid + 1)
                        turn(side1, lambda m: normed[1][:, m, :]).then_inc(u_turned, 1)
                    if ph.at.get("attn") == t:
                        if ph.steady_b:
                            pe.wait_ge(cw_done[q], ph.prep[0] + 1)
                        attention(ph.mid)

            pe.wait_ge(consts_set, 1)
            keep_busy(WARM_START, side0, zeros_r[:, :], g_hi[:, 0, :])
            pe.wait_ge(small_in[0], 48)
            turn_x(0, 0, 0, 0)
            keep_busy(WARM_ROWS, side0, zeros_r[:, :], g_hi[:, 0, :])
            pe.wait_ge(ce_lo_done, 1)
            affinities(0, 0)
            over_phases(pe, phase)
            for t in range(SLOTS - LAG, NT):
                down_product(Phase(2 * B - 1, 1, {}), t)
            pe.wait_ge(out_done, B - 1)
            for h in range(2):
                pe.wait_ge(y_copied, 2 * B + h)
                for m in range(h * NB // 2, (h + 1) * NB // 2):
                    last = nc.tensor.transpose(rows((side0, side1)[h], m), rows(y_sb, m), ident[:, :])
                last.then_inc(y_turned, 1)


def kernel(L0_attn_u, L0_attn_WA, L0_attn_WB, L0_attn_WAf, L0_attn_WBf, L0_attn_w1, L0_attn_w2, L0_attn_b, L0_attn_Wc,
           L0_ffn_centroids, L0_ffn_expert_biases, L0_ffn_Ws_up, L0_ffn_Ws_down, L0_ffn_W_up, L0_ffn_W_down):
    import numpy as np
    import concourse.bacc as bacc
    from concourse.bass_utils import run_bass_kernel_spmd

    def lay(a):
        return np.ascontiguousarray(a)

    WB, WBf = np.asarray(L0_attn_WB), np.asarray(L0_attn_WBf)
    w_up = np.asarray(L0_ffn_W_up).reshape(E, D, NJ, R).transpose(1, 2, 0, 3).reshape(D, NJ, P)
    w_down = np.asarray(L0_ffn_W_down).reshape(E, NJ, R, D).transpose(0, 2, 1, 3).reshape(P, NJ, D)
    arrays = {
        "x": lay(L0_attn_u), "ident": np.eye(P, dtype=np.float32), "cent_t": lay(np.asarray(L0_ffn_centroids).T),
        "ebias": lay(L0_ffn_expert_biases), "ws_up": lay(L0_ffn_Ws_up), "ws_down": lay(L0_ffn_Ws_down),
        "w_up": lay(w_up), "w_down": lay(w_down), "wb": lay(WB), "wb_t": lay(WB.T), "wbf": lay(WBf), "wbf_t": lay(WBf.T),
        "w1": lay(np.asarray(L0_attn_w1).reshape(D, 1)), "w2": lay(np.asarray(L0_attn_w2).reshape(D, 1)),
        "b": lay(L0_attn_b),
    }
    nc = bacc.Bacc("TRN2", target_bir_lowering=False, num_devices=1)
    args = [nc.dram_tensor(f"in_{k}", a.shape, mybir.dt.from_np(a.dtype), kind="ExternalInput").ap() for k, a in arrays.items()]
    out = nc.dram_tensor("out_0", (B, T, D), mybir.dt.float32, kind="ExternalOutput").ap()
    build(nc, *args, out)
    r = run_bass_kernel_spmd(nc, [{f"in_{k}": a for k, a in arrays.items()}], core_ids=[0])
    return r.results[0]["out_0"]
```
